# Optimizing a Trainium2 kernel written in Bass

```python
import numpy as np
import jax
import jax.numpy as jnp

def _softmax(x, axis=-1):
    return jax.nn.softmax(x, axis=axis)

def _gelu(x):
    return jax.nn.gelu(x, approximate=True)

def _silu(x):
    return jax.nn.silu(x)

def _sigmoid(x):
    return jax.nn.sigmoid(x)

def _layernorm(x, axis=-1, eps=1e-05):
    m = jnp.mean(x, axis=axis, keepdims=True)
    v = jnp.var(x, axis=axis, keepdims=True)
    return (x - m) / jnp.sqrt(v + eps)

def _scatter_add(tgt, idx, src, axis=0):
    return tgt.at[idx].add(src)

def _segment_sum(src, seg, n):
    return jax.ops.segment_sum(src, seg, n)
kernel_name = 'mk_prb_d1_jaxref_r8_a6d265'

def setup_inputs(seed: int=0):
    np.random.seed(seed)
    _w = jnp.asarray

    def _L0_attn_setup():
        import jax, jax.numpy as jnp
        import numpy as np
        DIM = 128
        HEADS = 16
        DIM_HEAD = DIM // HEADS
        LATENT = DIM // 4
        SCALE = DIM_HEAD ** (-0.5)
        key = jax.random.key(seed)
        ks = jax.random.split(key, 8)
        B, S = (2, 256)
        init = lambda k, shape, fan_in: jax.random.normal(k, shape, jnp.float32) * fan_in ** (-0.5)
        return {'x': jax.random.normal(ks[0], (B, S, DIM), jnp.float32), 'Wq': init(ks[1], (DIM, DIM), DIM), 'bq': jnp.zeros((DIM,), jnp.float32), 'Wl': init(ks[2], (DIM, LATENT), DIM), 'bl': jnp.zeros((LATENT,), jnp.float32), 'Wk': init(ks[3], (LATENT, DIM), LATENT), 'bk': jnp.zeros((DIM,), jnp.float32), 'Wv': init(ks[4], (LATENT, DIM), LATENT), 'bv': jnp.zeros((DIM,), jnp.float32), 'Wo': init(ks[5], (DIM, DIM), DIM), 'bo': jnp.zeros((DIM,), jnp.float32)}
    _L0_attn_in = _L0_attn_setup()

    def _L0_ffn_setup():
        import jax, jax.numpy as jnp
        import numpy as np
        H = 8
        QD = 32
        HALF = QD // 2
        DIMS = (32, 32)
        TOPK = 16
        DTK = 4
        EPS_BN = 1e-05
        EPS_NORM = 1e-12

        def _l2norm(x):
            n = jnp.linalg.norm(x, axis=-1, keepdims=True)
            return x / jnp.maximum(n, EPS_NORM)
        key = jax.random.key(seed)
        ks = jax.random.split(key, 6)
        B, S, D, O, E = (2, 64, 128, 128, 128)
        hidden_states = jax.random.normal(ks[0], (B, S, D), jnp.float32)
        Wq = jax.random.normal(ks[1], (D, H * QD), jnp.float32) * 0.02
        bq = jnp.zeros((H * QD,), jnp.float32)
        bn_gamma = jnp.ones((QD,), jnp.float32)
        bn_beta = jnp.zeros((QD,), jnp.float32)
        sub_key0 = jax.random.normal(ks[2], (DIMS[0], HALF), jnp.float32) * 0.02
        sub_key1 = jax.random.normal(ks[3], (DIMS[1], HALF), jnp.float32) * 0.02
        expert_down = jax.random.normal(ks[4], (E, D), jnp.float32) * 0.02
        expert_up = jax.random.normal(ks[5], (E, O), jnp.float32) * 0.02
        return {'hidden_states': hidden_states, 'Wq': Wq, 'bq': bq, 'bn_gamma': bn_gamma, 'bn_beta': bn_beta, 'sub_key0': sub_key0, 'sub_key1': sub_key1, 'expert_down': expert_down, 'expert_up': expert_up}
    _L0_ffn_in = _L0_ffn_setup()
    _d = {'L0_attn_x': _L0_attn_in['x'], 'L0_attn_Wq': _L0_attn_in['Wq'], 'L0_attn_bq': _L0_attn_in['bq'], 'L0_attn_Wl': _L0_attn_in['Wl'], 'L0_attn_bl': _L0_attn_in['bl'], 'L0_attn_Wk': _L0_attn_in['Wk'], 'L0_attn_bk': _L0_attn_in['bk'], 'L0_attn_Wv': _L0_attn_in['Wv'], 'L0_attn_bv': _L0_attn_in['bv'], 'L0_attn_Wo': _L0_attn_in['Wo'], 'L0_attn_bo': _L0_attn_in['bo'], 'L0_ffn_Wq': _L0_ffn_in['Wq'], 'L0_ffn_bq': _L0_ffn_in['bq'], 'L0_ffn_bn_gamma': _L0_ffn_in['bn_gamma'], 'L0_ffn_bn_beta': _L0_ffn_in['bn_beta'], 'L0_ffn_sub_key0': _L0_ffn_in['sub_key0'], 'L0_ffn_sub_key1': _L0_ffn_in['sub_key1'], 'L0_ffn_expert_down': _L0_ffn_in['expert_down'], 'L0_ffn_expert_up': _L0_ffn_in['expert_up']}
    _x0 = _d['L0_attn_x']
    _d['L0_attn_x'] = jax.random.normal(jax.random.fold_in(jax.random.key(seed), 1), (16, 256, 128), dtype=_x0.dtype)
    del _x0
    return _d

def reference(L0_attn_x, L0_attn_Wq, L0_attn_bq, L0_attn_Wl, L0_attn_bl, L0_attn_Wk, L0_attn_bk, L0_attn_Wv, L0_attn_bv, L0_attn_Wo, L0_attn_bo, L0_ffn_Wq, L0_ffn_bq, L0_ffn_bn_gamma, L0_ffn_bn_beta, L0_ffn_sub_key0, L0_ffn_sub_key1, L0_ffn_expert_down, L0_ffn_expert_up):

    def _L0_attn_ref(x, Wq, bq, Wl, bl, Wk, bk, Wv, bv, Wo, bo):
        import jax, jax.numpy as jnp
        import numpy as np
        DIM = 128
        HEADS = 16
        DIM_HEAD = DIM // HEADS
        LATENT = DIM // 4
        SCALE = DIM_HEAD ** (-0.5)
        B, S, D = x.shape
        H, Dh = (HEADS, DIM_HEAD)
        q = (x @ Wq + bq).reshape(B, S, H, Dh)
        latent = x @ Wl + bl
        k = (latent @ Wk + bk).reshape(B, S, H, Dh)
        v = (latent @ Wv + bv).reshape(B, S, H, Dh)
        scores = jnp.einsum('bihd,bjhd->bhij', q, k) * SCALE
        attn = jax.nn.softmax(scores, axis=-1)
        out = jnp.einsum('bhij,bjhd->bihd', attn, v).reshape(B, S, D)
        out = out @ Wo + bo
        return out

    def _L0_ffn_ref(hidden_states, Wq, bq, bn_gamma, bn_beta, sub_key0, sub_key1, expert_down, expert_up):
        import jax, jax.numpy as jnp
        import numpy as np
        H = 8
        QD = 32
        HALF = QD // 2
        DIMS = (32, 32)
        TOPK = 16
        DTK = 4
        EPS_BN = 1e-05
        EPS_NORM = 1e-12

        def _l2norm(x):
            n = jnp.linalg.norm(x, axis=-1, keepdims=True)
            return x / jnp.maximum(n, EPS_NORM)
        B, S, D = hidden_states.shape
        q = (hidden_states @ Wq + bq).reshape(B, S, H, QD)
        mean = q.mean(axis=(0, 1, 2))
        var = q.var(axis=(0, 1, 2))
        q = (q - mean) / jnp.sqrt(var + EPS_BN) * bn_gamma + bn_beta
        q0 = _l2norm(q[..., :HALF])
        q1 = _l2norm(q[..., HALF:])
        k0 = _l2norm(sub_key0)
        k1 = _l2norm(sub_key1)
        s0 = jnp.einsum('bshq,kq->bshk', q0, k0)
        s1 = jnp.einsum('bshq,kq->bshk', q1, k1)
        ts0, ti0 = jax.lax.top_k(s0, DTK)
        ts1, ti1 = jax.lax.top_k(s1, DTK)
        comb_s = (ts0[..., :, None] + ts1[..., None, :]).reshape(B, S, H, DTK * DTK)
        comb_i = (ti0[..., :, None] * DIMS[1] + ti1[..., None, :]).reshape(B, S, H, DTK * DTK)
        top_s, pos = jax.lax.top_k(comb_s, TOPK)
        idx = jnp.take_along_axis(comb_i, pos, axis=-1)
        w = jax.nn.softmax(top_s, axis=-1)
        down = expert_down[idx]
        up = expert_up[idx]
        eh = jnp.einsum('bshkd,bsd->bshk', down, hidden_states)
        eh = jax.nn.gelu(eh, approximate=False)
        out = jnp.einsum('bshko,bshk->bso', up, eh * w)
        return out
    x = L0_attn_x
    xn = _layernorm(x, axis=-1)
    x = x + _L0_attn_ref(xn, L0_attn_Wq, L0_attn_bq, L0_attn_Wl, L0_attn_bl, L0_attn_Wk, L0_attn_bk, L0_attn_Wv, L0_attn_bv, L0_attn_Wo, L0_attn_bo) + _L0_ffn_ref(xn, L0_ffn_Wq, L0_ffn_bq, L0_ffn_bn_gamma, L0_ffn_bn_beta, L0_ffn_sub_key0, L0_ffn_sub_key1, L0_ffn_expert_down, L0_ffn_expert_up)
    return x

_drawn_inputs = setup_inputs


def setup_inputs(seed=0):
    import zlib

    import numpy as np

    out = dict(_drawn_inputs(seed))
    spreads = {'L0_attn_bq': (0.0, 0.492),
     'L0_attn_bl': (0.0, 0.1),
     'L0_attn_bk': (0.0, 0.8),
     'L0_attn_bv': (0.0, 0.1),
     'L0_attn_bo': (0.0, 0.1),
     'L0_ffn_bq': (0.0, 0.8),
     'L0_ffn_bn_gamma': (1.0, 0.6),
     'L0_ffn_bn_beta': (0.0, 0.8)}
    factors = {'L0_ffn_Wq': 8.0,
     'L0_ffn_sub_key0': 8.0,
     'L0_ffn_sub_key1': 8.0,
     'L0_ffn_expert_down': 3.389,
     'L0_ffn_expert_up': 3.475}
    for name, (base, spread) in spreads.items():
        noise = np.random.default_rng([zlib.crc32(name.encode()), seed]).standard_normal(out[name].shape)
        drawn = base * np.exp(spread * noise) if base else spread * noise
        out[name] = jnp.asarray(drawn.astype(out[name].dtype))
    for name, factor in factors.items():
        out[name] = (out[name] * factor).astype(out[name].dtype)
    return out
```

```python
from contextlib import ExitStack

import numpy as np

import concourse.bass as bass
from concourse import mybir

F32 = mybir.dt.float32
BF16 = mybir.dt.bfloat16
ALU = mybir.AluOpType
ACT = mybir.ActivationFunctionType
AX = mybir.AxisListType.X

P = 128
NEG = -1.0e20

C_ID, C_SEL, C_AVG, C_GRP = 0, 128, 164, 292
C_END = 300


def constants():
    c = np.zeros((P, C_END), np.float32)
    p = np.arange(P)
    c[p, C_ID + p] = 1.0
    for col in range(4):
        for r in range(9):
            c[32 * col + r, C_SEL + 9 * col + r] = 1.0
    c[:, C_AVG:C_AVG + P] = (p[:, None] % 32 == p[None, :] % 32) / 8.0
    c[p, C_GRP + p // 16] = 1.0
    return c


def program(nc, x, Wq, bq, Wl, bl, Wk, bk, Wv, bv, Wo, bo,
            fWq, fbq, gamma, beta, key0, key1, down, up, const, scratch, out):
    B, S, D = x.shape
    T = B * S
    NT = T // P
    CH = 512
    NC = T // CH
    TC = CH // P
    BT = S // P
    L = Wl.shape[1]
    H, DH = 16, 8
    NPAIR = H // 2
    SCALE = float(DH) ** -0.5
    VC = DH + 1
    FH, FQ = 8, 32
    G = 2 * FH
    NK = 32
    TOP = 4
    KP = NK + TOP
    E = down.shape[0]
    ROWS = 48
    MROWS = 50
    Q_PART = (0, 0, 0, 1, 1, 2)
    K_PART = (0, 1, 2, 0, 1, 0)
    LN_EPS, BN_EPS, NORM_EPS = 1e-5, 1e-5, 1e-12

    xt = x.rearrange("b (n p) d -> p (b n) d", p=P)
    ot = out.rearrange("b (n p) d -> p (b n) d", p=P)

    ctx = ExitStack()
    with ctx:
        def sb(name, shape, dt=F32):
            return ctx.enter_context(nc.sbuf_tensor(name, shape, dt))

        def sem(name):
            return ctx.enter_context(nc.semaphore(name))

        cst = sb("cst", [P, C_END])
        ident = cst[:, C_ID:C_ID + P]
        sel = cst[:, C_SEL:C_SEL + 36]
        avg = cst[:, C_AVG:C_AVG + P]
        grp = cst[:, C_GRP:C_GRP + 8]
        ident_b = sb("ident_b", [P, P], BF16)
        wq_sb = sb("wq_sb", [P, D]); wl_sb = sb("wl_sb", [P, L]); wk_sb = sb("wk_sb", [L, D])
        wv_sb = sb("wv_sb", [L + 1, D]); wo_sb = sb("wo_sb", [P, D])
        fwq_sb = sb("fwq_sb", [P, 2 * P]); down_sb = sb("down_sb", [P, D]); up_sb = sb("up_sb", [P, D])
        downT = sb("downT", [P, E])
        bo_sb = sb("bo_sb", [P, D])
        cols = sb("cols", [P, 8])
        keys = sb("keys", [NK, 2, 16])
        keys_sq = sb("keys_sq", [NK, 2, 16])
        keys_n = sb("keys_n", [NK, 2, 3])
        keys_rep = sb("keys_rep", [NK, 4, 2, 16])
        kblk = sb("kblk", [P, 8, NK])
        x_sb = sb("x_sb", [P, NT, D])
        xn_sb = sb("xn_sb", [P, 2, TC, D])
        xnT = sb("xnT", [P, T])
        st6 = sb("st6", [P, NT, 6]); mv = sb("mv", [P, NT, 2])
        ve = sb("ve", [P, NT]); sd = sb("sd", [P, NT]); rs = sb("rs", [P, NT])
        lat = sb("lat", [L + 1, 2, CH])
        vhat = sb("vhat", [P, NT * H * VC + 32])
        q32 = sb("q32", [P, 2, CH]); r32 = sb("r32", [P, 2, CH])
        parts = sb("parts", [P, 2, 3, CH], BF16)
        fst = sb("fst", [P, 2, NC, 6]); fmv = sb("fmv", [P, 2, 2])
        bnv = sb("bnv", [P, 16])
        gT = xnT
        fqT = sb("fqT", [P, 2, T])
        sq = sb("sq", [P, 2, CH])
        rn = sb("rn", [P, NT, G])
        rn_t = sb("rn_t", [P, NT, G])
        QS = sb("QS", [P, 2, NPAIR, CH], BF16)
        KS = sb("KS", [P, 2, NPAIR, CH], BF16)
        negm = sb("negm", [P, 2, 2, 2, BT, NPAIR])
        mpart = sb("mpart", [P, BT, 2, 2, NPAIR], BF16)
        mT = sb("mT", [2 * H, S], BF16)
        Eb = sb("Eb", [P, 4, 2, BT, S])
        Osb = sb("Osb", [P, 4, S])
        rden = sb("rden", [P, BT, H]); on = sb("on", [P, BT, D]); onT = sb("onT", [P, S])
        ysb = sb("ysb", [P, 2, BT, D])
        s_sb = sb("s_sb", [P, BT * G, KP]); r_sb = sb("r_sb", [P, BT * G, KP])
        z_sb = sb("z_sb", [P, BT * G, KP])
        top8 = sb("top8", [P, BT * G, 8]); top4 = sb("top4", [P, BT * G, 8])
        den = sb("den", [P, BT * G]); dinv = sb("dinv", [P, BT * G])
        rest = sb("rest", [P, BT * FH]); dd = sb("dd", [P, BT * FH]); a0 = sb("a0", [P, BT * FH, TOP])
        restn = sb("restn", [P, BT]); restm = sb("restm", [P, BT * FH])
        prod = sb("prod", [P, BT, FH, TOP, NK])
        wsum = sb("wsum", [P, BT, E])
        wgT = sb("wgT", [P, S])

        bank = [ctx.enter_context(nc.psum_tensor(f"bank{i}", [P, 512], F32)) for i in range(4)]
        SJ = [ctx.enter_context(nc.psum_tensor(f"SJ{i}", [P, 1024], F32)) for i in range(2)]
        psX = [bank[0], bank[1]]
        psQ, psL = bank[2], bank[3]
        psK, psV = SJ[0][:, 0:512], SJ[0][:, 512:1024]
        psF = [SJ[1][:, 0:512], SJ[1][:, 512:1024]]
        SI = [bank[0], bank[1]]
        psO, psM = bank[2], bank[3]

        names = ("w x0 x1 x2 x3 x4 x5 x6 x7 w2 stats var std rstd xn xT xnT q q_ev l l_ev k k_ev v v_ev f f_st "
                 "hi_q hi_k r_q r_k mid_q mid_k lo_q lo_k spill kn1 kn2 kn3 kn4 kn5 krep kmm kblk dT downT "
                 "bn ba bb bc g g_ev ff ff_ev sq n2 n2s n2c rn latone ones misc_c identb "
                 "si mx ms mt mt_ev mrow sj ex pv o_ev ct rd on onp onT y fin st0 st1 "
                 "fs fs_ev t8 t4 mr z ze es fd fe ff1 fg fa pr ws wx wt wg xb load0 load1 vone").split()
        s = {n: sem("s_" + n) for n in names}

        block = ctx.enter_context(nc.Block())
        NSLOT = 8 * B + 24

        WLOADS = [(cst[:, :], const), (wq_sb[:, :], Wq), (wl_sb[:, :], Wl), (wk_sb[:, :], Wk),
                  (wv_sb[0:L, :], Wv), (wv_sb[L:L + 1, :], bv.rearrange("(a n) -> a n", a=1)),
                  (fwq_sb[:, :], fWq), (cols[:, 0:1], bq.rearrange("(p a) -> p a", a=1)),
                  (cols[:, 1:2], bk.rearrange("(p a) -> p a", a=1)),
                  (cols[:, 4:5], fbq[0:P].rearrange("(p a) -> p a", a=1)),
                  (cols[:, 5:6], fbq[P:2 * P].rearrange("(p a) -> p a", a=1)),
                  (cols[0:L, 6:7], bl.rearrange("(p a) -> p a", a=1))]
        for i in range(4):
            WLOADS += [(cols[32 * i:32 * i + 32, 2:3], gamma.rearrange("(p a) -> p a", a=1)),
                       (cols[32 * i:32 * i + 32, 3:4], beta.rearrange("(p a) -> p a", a=1))]
        W2LOADS = [(wo_sb[:, :], Wo), (down_sb[:, :], down), (up_sb[:, :], up),
                   (keys[:, 0, :], key0), (keys[:, 1, :], key1),
                   (bo_sb[:, :], bo.rearrange("(a n) -> a n", a=1).to_broadcast([P, D]))]
        NW, NW2 = 16 * len(WLOADS), 16 * len(W2LOADS)

        @block.sync
        def _(sp):
            for c in range(NC):
                sp.dma_start(x_sb[:, TC * c:TC * (c + 1), :], xt[:, TC * c:TC * (c + 1), :]).then_inc(s[f"x{c}"], 16)
            for dst, src in W2LOADS:
                sp.dma_start(dst, src).then_inc(s["w2"], 16)
            for c in range(NC):
                for t in range(2):
                    sp.wait_ge(s["lo_q" if t == 0 else "lo_k"], c + 1)
                    sp.dma_start(scratch[t, :, :, c * CH:(c + 1) * CH].rearrange("a p n -> p a n"),
                                 parts[:, t, :, :]).then_inc(s["spill"], 16)
            def store(b):
                sp.wait_ge(s["fin"], b + 1)
                sp.dma_start(ot[:, BT * b:BT * (b + 1), :], ysb[:, b % 2, :, :]).then_inc(s[f"st{b % 2}"], 16)

            stored = 0
            sp.wait_ge(s["ones"], 1)
            for c in range(NC):
                sp.wait_ge(s["spill"], 32 * (c + 1))
                while stored < 2 * c - 3:
                    store(stored)
                    stored += 1
                if c >= 2:
                    sp.wait_ge(s["sj"], NPAIR * 2 * (c - 1))
                for t, dst, plist in ((0, QS, Q_PART), (1, KS, K_PART)):
                    view = scratch[t, :, :, c * CH:(c + 1) * CH].rearrange("a (r e d) n -> a e d r n", e=2, d=DH)
                    for e in range(2):
                        for term, part in enumerate(plist):
                            r0 = 64 * e + DH * term
                            sp.dma_start(dst[r0:r0 + DH, c % 2, :, :], view[part, e]).then_inc(s[f"load{c % 2}"], 16)
            for b in range(stored, B):
                store(b)
            for e in range(2):
                sp.wait_ge(s[f"st{e}"], 16 * B // 2)

        LOADS = 16 * 24

        def chunk_loaded(eng, c):
            eng.wait_ge(s[f"load{c % 2}"], LOADS * (c // 2 + 1))

        @block.scalar
        def _(act):
            for dst, src in WLOADS:
                act.dma_start(dst, src).then_inc(s["w"], 16)
            act.wait_ge(s["var"], 1)
            nc.scalar.activation(sd[:, :], ve[:, :], ACT.Sqrt).then_inc(s["std"], 1)
            act.wait_ge(s["kn2"], 1)
            nc.scalar.activation(keys_n[:, :, 1], keys_n[:, :, 0], ACT.Sqrt).then_inc(s["kn3"], 1)
            act.wait_ge(s["w"], NW)
            for c in range(NC + 1):
                if c < NC:
                    act.wait_ge(s["xT"], c + 1)
                    nc.scalar.activation(xnT[:, c * CH:(c + 1) * CH], psX[c % 2][:, :], ACT.Copy).then_inc(s["xnT"], 1)
                    act.wait_ge(s["l"], c + 1)
                    if c >= 2:
                        act.wait_ge(s["v"], c - 1)
                    nc.scalar.activation(lat[0:L, c % 2, :], psL[0:L, :], ACT.Identity,
                                         bias=cols[0:L, 6:7]).then_inc(s["l_ev"], 1)
                    act.wait_ge(s["v"], c + 1)
                    act.wait_ge(s["vone"], 1)
                    nc.scalar.activation(
                        vhat[:, TC * c * H * VC:TC * (c + 1) * H * VC].rearrange("p (n v) -> p n v", v=VC)[:, :, 0:DH],
                        psV.rearrange("p (n v) -> p n v", v=DH), ACT.Copy).then_inc(s["v_ev"], 1)
                    for t, nm in enumerate(("q", "k")):
                        if c >= 1:
                            act.wait_ge(s["spill"], 32 * c)
                        act.wait_ge(s[nm + "_ev"], c + 1)
                        nc.scalar.activation(parts[:, t, 0, :], q32[:, t, :], ACT.Copy).then_inc(s["hi_" + nm], 1)
                        act.wait_ge(s["r_" + nm], c + 1)
                        nc.scalar.activation(parts[:, t, 1, :], r32[:, t, :], ACT.Copy).then_inc(s["mid_" + nm], 1)
            act.wait_ge(s["bc"], 1)
            nc.scalar.activation(bnv[:, 6:7], bnv[:, 5:6], ACT.Sqrt).then_inc(s["bc"], 1)
            act.wait_ge(s["bn"], 1)
            for i in range(2 * NC):
                c, r = i // 2, i % 2
                act.wait_ge(s["ff"], i + 1)
                nc.scalar.activation(fqT[:, r, c * CH:(c + 1) * CH], psF[i % 2], ACT.Identity,
                                     bias=bnv[:, 8 + r:9 + r], scale=bnv[:, 7:8]).then_inc(s["ff_ev"], 1)
            act.wait_ge(s["n2"], NC)
            nc.scalar.activation(rn_t[:, :, :], psQ[:, :].rearrange("p (n g) -> p n g", g=G), ACT.Sqrt).then_inc(s["n2s"], 1)
            for c in range(NC):
                act.wait_ge(s["g"], c + 1)
                nc.scalar.activation(gT[:, c * CH:(c + 1) * CH], psX[c % 2][:, :], ACT.Gelu).then_inc(s["g_ev"], 1)

            for slot in range(NSLOT):
                k = slot % 8
                b = slot // 8 - 1
                if k == 0 and 0 <= b < B:
                    act.wait_ge(s["mt"], b + 1)
                    if b >= 1:
                        act.wait_ge(s["mrow"], 64 * b)
                    nc.scalar.activation(mT[:, :], psM[0:2 * H, 0:S], ACT.Copy).then_inc(s["mt_ev"], 1)
                    for e in range(2):
                        for part in range(2):
                            src = (part * 2 + e) * NPAIR
                            r0 = 64 * e + ROWS + part
                            act.wait_ge(s["mt_ev"], b + 1)
                            act.dma_start(QS[r0:r0 + 1, (b // 2) % 2, :, (b % 2) * S:(b % 2 + 1) * S],
                                          mT[src:src + NPAIR, :]).then_inc(s["mrow"], 16)
                if k in (1, 2) and 0 <= b < B:
                    t = k - 1
                    act.wait_ge(s["fs"], 2 * b + t + 1)
                    if b >= 1:
                        act.wait_ge(s["mr"], 2 * b)
                        act.wait_ge(s["z"], 2 * b)
                    nc.scalar.activation(s_sb[:, G * t:G * (t + 1), 0:NK],
                                         psM[:, :].rearrange("p (g k) -> p g k", k=NK), ACT.Copy).then_inc(s["fs_ev"], 1)
                if k == 5 and 0 <= b < B:
                    act.wait_ge(s["z"], 2 * b + 2)
                    nc.scalar.activation(z_sb[:, :, :], z_sb[:, :, :], ACT.Exp).then_inc(s["ze"], 1)
                n = slot - 12
                if 0 <= n < NPAIR * B:
                    act.wait_ge(s["sj"], n + 1)
                    if n >= 4:
                        act.wait_ge(s["pv"], (n - 4) // 2 + 1)
                    nc.scalar.activation(Eb[:, n % 4, :, :, :].rearrange("p h j i -> p (h j i)"), SJ[n % 2][:, :],
                                         ACT.Exp).then_inc(s["ex"], 1)
                m = slot - 14
                if m >= 0 and m % 2 == 0 and m // 2 < 4 * B:
                    g = m // 2
                    act.wait_ge(s["pv"], g + 1)
                    if g >= 4:
                        act.wait_ge(s["ct"], g // 4)
                    nc.scalar.activation(Osb[:, g % 4, :], psO[:, (g % 2) * S:(g % 2 + 1) * S], ACT.Copy).then_inc(s["o_ev"], 1)
                b = (slot - 22) // 8
                if k == 6 and 0 <= b < B:
                    act.wait_ge(s["onp"], b + 1)
                    if b >= 1:
                        act.wait_ge(s["y"], b)
                    nc.scalar.activation(onT[:, :], psM[:, 0:S], ACT.Copy).then_inc(s["onT"], 1)

        @block.tensor
        def _(pe):
            mm = nc.tensor.matmul
            pe.wait_ge(s["w"], NW)
            pe.wait_ge(s["latone"], 1)
            for c in range(NC):
                pe.wait_ge(s["xn"], c + 1)
                if c >= 2:
                    pe.wait_ge(s["xnT"], c - 1)
                for t in range(TC):
                    last = mm(psX[c % 2][:, t * P:(t + 1) * P], xn_sb[:, c % 2, t, :], ident, start=True, stop=True)
                last.then_inc(s["xT"], 1)
                pe.wait_ge(s["xnT"], c + 1)
                xc = xnT[:, c * CH:(c + 1) * CH]
                if c >= 1:
                    pe.wait_ge(s["l_ev"], c)
                mm(psL[0:L, :], wl_sb[:, :], xc, start=True, stop=True).then_inc(s["l"], 1)
                if c >= 1:
                    pe.wait_ge(s["q_ev"], c)
                mm(psQ[:, :], wq_sb[:, :], xc, start=True, stop=True).then_inc(s["q"], 1)
                for r in range(2):
                    if c >= 1:
                        pe.wait_ge(s["f_st"], 2 * (c - 1) + r + 1)
                    mm(psF[r], fwq_sb[:, r * P:(r + 1) * P], xc, start=True, stop=True).then_inc(s["f"], 1)
                pe.wait_ge(s["l_ev"], c + 1)
                if c >= 1:
                    pe.wait_ge(s["v_ev"], c)
                    pe.wait_ge(s["k_ev"], c)
                mm(psK, wk_sb[:, :], lat[0:L, c % 2, :], start=True, stop=True).then_inc(s["k"], 1)
                for t in range(TC):
                    last = mm(psV[:, t * P:(t + 1) * P], lat[:, c % 2, t * P:(t + 1) * P], wv_sb[:, :], start=True, stop=True)
                last.then_inc(s["v"], 1)
            pe.wait_ge(s["krep"], 1)
            pe.wait_ge(s["q_ev"], NC)
            mm(psQ[:, 0:NK], keys_rep[:, :, :, :].rearrange("k h a d -> k (h a d)"), cst[0:NK, 0:NK], start=True, stop=True)\
                .then_inc(s["kmm"], 1)
            pe.wait_ge(s["w2"], NW2)
            pe.wait_ge(s["l_ev"], NC)
            mm(psL[:, 0:E], down_sb[:, :], ident, start=True, stop=True).then_inc(s["dT"], 1)
            pe.wait_ge(s["ba"], 1)
            pe.wait_ge(s["downT"], 1)
            for r in range(2):
                last = mm(psL[:, 0:1], avg, bnv[:, r:r + 1], start=(r == 0), stop=(r == 1))
            last.then_inc(s["ba"], 1)
            pe.wait_ge(s["bb"], 1)
            for r in range(2):
                last = mm(psL[:, 2:3], avg, bnv[:, 2 + r:3 + r], start=(r == 0), stop=(r == 1))
            last.then_inc(s["bb"], 1)
            pe.wait_ge(s["kblk"], 1)
            for c in range(NC):
                xc = xnT[:, c * CH:(c + 1) * CH]
                for r in range(2):
                    i = 2 * c + r
                    if i >= 2:
                        pe.wait_ge(s["ff_ev"], i - 1)
                    else:
                        pe.wait_ge(s["f_st"], 2 * NC)
                    mm(psF[r], fwq_sb[:, r * P:(r + 1) * P], xc, start=True, stop=True).then_inc(s["ff"], 1)
                for cc in ([c - 1] if c >= 1 else []) + ([c] if c == NC - 1 else []):
                    pe.wait_ge(s["sq"], cc + 1)
                    for t in range(TC):
                        for r in range(2):
                            o = (cc * TC + t) * G + 8 * r
                            last = mm(psQ[:, o:o + 8], sq[:, r, t * P:(t + 1) * P], grp, start=True, stop=True)
                    last.then_inc(s["n2"], 1)
            for c in range(NC):
                if c >= 2:
                    pe.wait_ge(s["g_ev"], c - 1)
                else:
                    pe.wait_ge(s["xnT"], NC)
                mm(psX[c % 2][:, :], downT[:, :], xnT[:, c * CH:(c + 1) * CH], start=True, stop=True).then_inc(s["g"], 1)
            pe.wait_ge(s["g_ev"], NC)
            pe.wait_ge(s["n2s"], 1)
            pe.wait_ge(s["v_ev"], NC)
            pe.wait_ge(s["k_ev"], NC)
            pe.wait_ge(s["bn"], 1)
            pe.wait_ge(s["identb"], 1)

            for slot in range(NSLOT):
                k = slot % 8
                n = slot
                if n < NPAIR * B:
                    b, pr = n // NPAIR, n % NPAIR
                    c, o = b // 2, (b % 2) * S
                    if pr == 0 and b % 2 == 0:
                        chunk_loaded(pe, c)
                    for e in range(2):
                        if n >= 1:
                            pe.wait_ge(s["mx"], 2 * (n - 1) + e + 1)
                        for t in range(BT):
                            last = mm(SI[e][:, t * S:(t + 1) * S],
                                      QS[64 * e:64 * e + ROWS, c % 2, pr, o + t * P:o + (t + 1) * P],
                                      KS[64 * e:64 * e + ROWS, c % 2, pr, o:o + S], start=True, stop=True)
                        last.then_inc(s["si"], 1)
                n = slot - 12
                if 0 <= n < NPAIR * B:
                    b, pr = n // NPAIR, n % NPAIR
                    c, o = b // 2, (b % 2) * S
                    if pr == 0:
                        pe.wait_ge(s["mrow"], 64 * (b + 1))
                    if n >= 2:
                        pe.wait_ge(s["ex"], n - 1)
                    else:
                        pe.wait_ge(s["ff_ev"], 2 * NC)
                    for e in range(2):
                        for t in range(BT):
                            last = mm(SJ[n % 2][:, (e * BT + t) * S:(e * BT + t + 1) * S],
                                      KS[64 * e:64 * e + MROWS, c % 2, pr, o + t * P:o + (t + 1) * P],
                                      QS[64 * e:64 * e + MROWS, c % 2, pr, o:o + S], start=True, stop=True)
                    last.then_inc(s["sj"], 1)
                b = slot // 8 - 1
                if k == 0 and 0 <= b < B:
                    pe.wait_ge(s["ms"], b + 1)
                    if b >= 2:
                        pe.wait_ge(s["fin"], b - 1)
                    for t in range(BT):
                        last = mm(psM[0:2 * H, t * P:(t + 1) * P], mpart[:, t, :, :, :].rearrange("p a e r -> p (a e r)"),
                                  ident_b[:, :], start=True, stop=True)
                    last.then_inc(s["mt"], 1)
                if k in (1, 2) and 0 <= b < B:
                    t = k - 1
                    if t == 0:
                        pe.wait_ge(s["mt_ev"], b + 1)
                    else:
                        pe.wait_ge(s["fs_ev"], 2 * b + 1)
                    tok = (BT * b + t) * P
                    for r in range(2):
                        last = mm(psM[:, 256 * r:256 * (r + 1)], fqT[:, r, tok:tok + P],
                                  kblk[:, :, :].rearrange("p g k -> p (g k)"), start=True, stop=True)
                    last.then_inc(s["fs"], 1)
                m = slot - 14
                if m >= 0 and m % 2 == 0 and m // 2 < 4 * B:
                    g = m // 2
                    b = g // 4
                    pe.wait_ge(s["ex"], 2 * g + 2)
                    if g >= 2:
                        pe.wait_ge(s["o_ev"], g - 1)
                    for t in range(BT):
                        for col in range(4):
                            h = 4 * (g % 4) + col
                            v0 = (BT * b + t) * H * VC + h * VC
                            last = mm(psO[32 * col:32 * col + 32, (g % 2) * S:(g % 2 + 1) * S], vhat[:, v0:v0 + 32],
                                      Eb[:, (2 * g + col // 2) % 4, col % 2, t, :], start=(t == 0), stop=(t == BT - 1),
                                      tile_position=(0, 32 * col), skip_group_check=True)
                    last.then_inc(s["pv"], 1)
                b = (slot - 20) // 8
                if k == 4 and 0 <= b < B:
                    pe.wait_ge(s["wx"], b + 1)
                    if b + 1 < B:
                        pe.wait_ge(s["fs_ev"], 2 * (b + 2))
                    for t in range(BT):
                        last = mm(psM[:, t * P:(t + 1) * P], wsum[:, t, :], ident, start=True, stop=True)
                    last.then_inc(s["wt"], 1)
                b = (slot - 21) // 8
                if k == 5 and 0 <= b < B:
                    pe.wait_ge(s["wg"], b + 1)
                    pe.wait_ge(s["o_ev"], 4 * (b + 1))
                    for t in range(BT):
                        for g in range(4):
                            last = mm(psM[:, t * 144 + 36 * g:t * 144 + 36 * (g + 1)], Osb[:, g, t * P:(t + 1) * P],
                                      sel, start=True, stop=True)
                    last.then_inc(s["ct"], 1)
                b = (slot - 22) // 8
                if k == 6 and 0 <= b < B:
                    pe.wait_ge(s["on"], b + 1)
                    for t in range(BT):
                        last = mm(psM[:, t * P:(t + 1) * P], on[:, t, :], ident, start=True, stop=True)
                    last.then_inc(s["onp"], 1)
                b = (slot - 23) // 8
                if k == 7 and 0 <= b < B:
                    pe.wait_ge(s["onT"], b + 1)
                    for t in range(BT):
                        mm(psM[:, t * D:(t + 1) * D], onT[:, t * P:(t + 1) * P], wo_sb[:, :], start=True, stop=False)
                        last = mm(psM[:, t * D:(t + 1) * D], wgT[:, t * P:(t + 1) * P], up_sb[:, :], start=False, stop=True)
                    last.then_inc(s["y"], 1)

        @block.vector
        def _(dve):
            V = nc.vector
            V.memset(vhat[:, :], 1.0).then_inc(s["vone"], 1)
            V.memset(KS[:, :, :, :].rearrange("p a r n -> p (a r n)"), 1.0).then_inc(s["ones"], 1)
            V.memset(s_sb[:, :, NK:KP], NEG)
            V.memset(top4[:, :, TOP:8], NEG).then_inc(s["misc_c"], 1)
            for c in range(NC):
                dve.wait_ge(s[f"x{c}"], 16)
                for n in range(TC * c, TC * (c + 1)):
                    last = V.bn_stats(st6[:, n, :], x_sb[:, n, :])
            last.then_inc(s["stats"], 1)
            dve.wait_ge(s["stats"], 1)
            for n in range(NT):
                last = V.bn_aggr(mv[:, n, :], st6[:, n, :])
            last.then_inc(s["stats"], 1)
            dve.wait_ge(s["stats"], 2)
            V.tensor_scalar(ve[:, :], mv[:, :, 1], LN_EPS, None, ALU.add).then_inc(s["var"], 1)
            dve.wait_ge(s["std"], 1)
            V.reciprocal(rs[:, :], sd[:, :]).then_inc(s["rstd"], 1)
            dve.wait_ge(s["rstd"], 1)
            dve.wait_ge(s["w"], NW)
            V.tensor_copy(ident_b[:, :], ident).then_inc(s["identb"], 1)
            for c in range(NC + 1):
                if c < NC:
                    if c >= 2:
                        dve.wait_ge(s["xT"], c - 1)
                    for t in range(TC):
                        n = TC * c + t
                        last = V.tensor_scalar(xn_sb[:, c % 2, t, :], x_sb[:, n, :], mv[:, n, 0:1], rs[:, n:n + 1],
                                               ALU.subtract, ALU.mult)
                    last.then_inc(s["xn"], 1)
                if c >= 1:
                    cc = c - 1
                    dve.wait_ge(s["q"], cc + 1)
                    if cc >= 1:
                        dve.wait_ge(s["r_q"], cc)
                        dve.wait_ge(s["hi_q"], cc)
                    V.tensor_scalar(q32[:, 0, :], psQ[:, :], cols[:, 0:1], SCALE, ALU.add, ALU.mult).then_inc(s["q_ev"], 1)
                    for r in range(2):
                        dve.wait_ge(s["f"], 2 * cc + r + 1)
                        V.bn_stats(fst[:, r, cc, :], psF[r]).then_inc(s["f_st"], 1)
                    dve.wait_ge(s["k"], cc + 1)
                    if cc >= 1:
                        dve.wait_ge(s["r_k"], cc)
                        dve.wait_ge(s["hi_k"], cc)
                    V.tensor_scalar(q32[:, 1, :], psK, cols[:, 1:2], None, ALU.add).then_inc(s["k_ev"], 1)
                if c == 0:
                    dve.wait_ge(s["w2"], NW2)
                    V.tensor_tensor(keys_sq[:, :, :], keys[:, :, :], keys[:, :, :], ALU.mult).then_inc(s["kn1"], 1)
                    dve.wait_ge(s["kn1"], 1)
                    V.tensor_reduce(keys_n[:, :, 0], keys_sq[:, :, :], axis=AX, op=ALU.add).then_inc(s["kn2"], 1)
                    dve.wait_ge(s["kn3"], 1)
                    V.tensor_scalar(keys_n[:, :, 2], keys_n[:, :, 1], NORM_EPS, None, ALU.max).then_inc(s["kn4"], 1)
                    dve.wait_ge(s["kn4"], 1)
                    V.reciprocal(keys_n[:, :, 0], keys_n[:, :, 2]).then_inc(s["kn5"], 1)
                    dve.wait_ge(s["kn5"], 1)
                    for h in range(4):
                        last = V.tensor_tensor(keys_rep[:, h, :, :], keys[:, :, :],
                                               keys_n[:, :, 0:1].to_broadcast([NK, 2, 16]), ALU.mult)
                    last.then_inc(s["krep"], 1)
            dve.wait_ge(s["kmm"], 1)
            V.tensor_tensor(kblk[:, :, :], psQ[:, 0:NK].unsqueeze(1).to_broadcast([P, 8, NK]),
                            grp.unsqueeze(2).to_broadcast([P, 8, NK]), ALU.mult).then_inc(s["kblk"], 1)
            dve.wait_ge(s["dT"], 1)
            V.tensor_copy(downT[:, :], psL[:, 0:E]).then_inc(s["downT"], 1)
            dve.wait_ge(s["f_st"], 2 * NC)
            for r in range(2):
                last = V.bn_aggr(fmv[:, r, :], fst[:, r, :, :])
            last.then_inc(s["misc_c"], 1)
            dve.wait_ge(s["misc_c"], 2)
            V.tensor_tensor(bnv[:, 0:2], fmv[:, :, 0], cols[:, 4:6], ALU.add).then_inc(s["ba"], 1)
            dve.wait_ge(s["ba"], 2)
            V.tensor_copy(bnv[:, 4:5], psL[:, 0:1]).then_inc(s["misc_c"], 1)
            dve.wait_ge(s["misc_c"], 3)
            V.tensor_scalar(bnv[:, 10:12], bnv[:, 0:2], bnv[:, 4:5], None, ALU.subtract).then_inc(s["misc_c"], 1)
            dve.wait_ge(s["misc_c"], 4)
            V.tensor_tensor(bnv[:, 12:14], bnv[:, 10:12], bnv[:, 10:12], ALU.mult).then_inc(s["misc_c"], 1)
            dve.wait_ge(s["misc_c"], 5)
            V.tensor_tensor(bnv[:, 2:4], bnv[:, 12:14], fmv[:, :, 1], ALU.add).then_inc(s["bb"], 1)
            dve.wait_ge(s["bb"], 2)
            V.tensor_scalar(bnv[:, 5:6], psL[:, 2:3], BN_EPS, None, ALU.add).then_inc(s["bc"], 1)
            dve.wait_ge(s["bc"], 2)
            V.reciprocal(bnv[:, 14:15], bnv[:, 6:7]).then_inc(s["misc_c"], 1)
            dve.wait_ge(s["misc_c"], 6)
            V.tensor_tensor(bnv[:, 7:8], bnv[:, 14:15], cols[:, 2:3], ALU.mult).then_inc(s["misc_c"], 1)
            V.tensor_scalar(bnv[:, 10:12], cols[:, 4:6], bnv[:, 4:5], None, ALU.subtract).then_inc(s["misc_c"], 1)
            dve.wait_ge(s["misc_c"], 8)
            V.tensor_scalar(bnv[:, 8:10], bnv[:, 10:12], bnv[:, 7:8], cols[:, 3:4], ALU.mult, ALU.add).then_inc(s["bn"], 1)
            dve.wait_ge(s["n2s"], 1)
            V.tensor_scalar(rn_t[:, :, :], rn_t[:, :, :], NORM_EPS, None, ALU.max).then_inc(s["n2c"], 1)
            dve.wait_ge(s["n2c"], 1)
            V.reciprocal(rn[:, :, :], rn_t[:, :, :]).then_inc(s["rn"], 1)

            for slot in range(NSLOT):
                k = slot % 8
                b = slot // 8 - 1
                if k == 0 and 0 <= b < B:
                    dve.wait_ge(s["mx"], 2 * NPAIR * (b + 1))
                    if b >= 1:
                        dve.wait_ge(s["mt"], b)
                    src = [negm[:, b % 2, j, :, :, :].rearrange("p e t r -> p t e r") for j in range(2)]
                    V.tensor_copy(mpart[:, :, 0, :, :], src[0]).then_inc(s["misc_c"], 1)
                    dve.wait_ge(s["misc_c"], 9 + b)
                    V.tensor_tensor(mpart[:, :, 1, :, :], src[0], mpart[:, :, 0, :, :], ALU.subtract).then_inc(s["ms"], 1)
                if slot < NPAIR * B:
                    bb, pr = slot // NPAIR, slot % NPAIR
                    for e in range(2):
                        dve.wait_ge(s["si"], 2 * slot + e + 1)
                        V.tensor_reduce(negm[:, bb % 2, 0, e, :, pr], SI[e][:, :].rearrange("p (t j) -> p t j", j=S),
                                        axis=AX, op=ALU.max, negate=True).then_inc(s["mx"], 1)
                if k in (2, 3) and 0 <= b < B:
                    t = k - 2
                    dve.wait_ge(s["fs_ev"], 2 * b + t + 1)
                    for g in range(G * t, G * (t + 1)):
                        last = V.max(top8[:, g, :], s_sb[:, g, 0:NK])
                    last.then_inc(s["t8"], 1)
                    dve.wait_ge(s["t8"], 2 * b + t + 1)
                    V.tensor_copy(top4[:, G * t:G * (t + 1), 0:TOP], top8[:, G * t:G * (t + 1), 0:TOP]).then_inc(s["t4"], 1)
                if k in (4, 5) and 0 <= b < B:
                    t = k - 4
                    dve.wait_ge(s["t4"], 2 * b + t + 1)
                    for g in range(G * t, G * (t + 1)):
                        last = V.match_replace(r_sb[:, g, :], top4[:, g, :], s_sb[:, g, :], NEG)
                    last.then_inc(s["mr"], 1)
                if k == 6 and 0 <= b < B:
                    dve.wait_ge(s["ze"], b + 1)
                    dve.wait_ge(s["mr"], 2 * b + 2)
                    if b >= 1:
                        dve.wait_ge(s["pr"], 2 * b)
                        dve.wait_ge(s["fg"], b)
                    V.tensor_reduce(den[:, :], z_sb[:, :, NK:KP], axis=AX, op=ALU.add).then_inc(s["fd"], 1)
                    V.scalar_tensor_tensor(r_sb[:, :, 0:NK], r_sb[:, :, 0:NK], NEG, z_sb[:, :, 0:NK],
                                           ALU.is_equal, ALU.mult).then_inc(s["es"], 1)
                    dve.wait_ge(s["fd"], b + 1)
                    V.reciprocal(dinv[:, :], den[:, :]).then_inc(s["fe"], 1)
                    dve.wait_ge(s["fe"], b + 1)
                    dve.wait_ge(s["es"], b + 1)
                    dh = dinv[:, :].rearrange("p (h a) -> p h a", a=2)
                    es = r_sb[:, :, :].rearrange("p (h a) k -> p h a k", a=2)
                    V.tensor_tensor(dd[:, :], dh[:, :, 0], dh[:, :, 1], ALU.mult).then_inc(s["ff1"], 1)
                    V.tensor_reduce(rest[:, :], es[:, :, 0, TOP:NK], axis=AX, op=ALU.add).then_inc(s["ff1"], 1)
                    dve.wait_ge(s["ff1"], 2 * b + 2)
                    V.tensor_tensor(a0[:, :, :], es[:, :, 0, 0:TOP],
                                    dd[:, :].unsqueeze(2).to_broadcast([P, BT * FH, TOP]), ALU.mult).then_inc(s["fa"], 1)
                    V.tensor_tensor(restm[:, :], rest[:, :], dh[:, :, 0], ALU.mult).then_inc(s["fg"], 1)
                b1 = (slot - 17) // 8
                if k in (1, 2) and slot >= 17 and b1 < B:
                    t = k - 1
                    b2 = (slot - 16) // 8
                    dve.wait_ge(s["pr"], 2 * b2 + t + 1)
                    if b2 >= 1:
                        dve.wait_ge(s["wt"], b2)
                    V.tensor_reduce(wsum[:, t, :], prod[:, t, :, :, :].rearrange("p h i j -> p (i j) h"),
                                    axis=AX, op=ALU.add).then_inc(s["ws"], 1)
                    if t == 1:
                        dve.wait_ge(s["fg"], b2 + 1)
                        V.tensor_reduce(restn[:, :], restm[:, :].rearrange("p (t h) -> p t h", t=BT), axis=AX,
                                        op=ALU.add).then_inc(s["ws"], 1)
                        dve.wait_ge(s["ws"], 3 * b2 + 3)
                        V.tensor_tensor(wsum[:, :, E - 1], wsum[:, :, E - 1], restn[:, :], ALU.add).then_inc(s["wx"], 1)
                b = (slot - 20) // 8
                if k == 4 and 0 <= b < B:
                    dve.wait_ge(s["wt"], b + 1)
                    if b >= 1:
                        dve.wait_ge(s["y"], b)
                    V.tensor_tensor(wgT[:, :], psM[:, 0:S], gT[:, b * S:(b + 1) * S], ALU.mult).then_inc(s["wg"], 1)
                b = (slot - 21) // 8
                if k == 5 and 0 <= b < B:
                    dve.wait_ge(s["ct"], b + 1)
                    ct = psM[:, 0:BT * 144].rearrange("p (t h v) -> p t h v", t=BT, v=VC)
                    if b >= 1:
                        dve.wait_ge(s["onp"], b)
                    V.reciprocal(rden[:, :, :], ct[:, :, :, DH]).then_inc(s["rd"], 1)
                    dve.wait_ge(s["rd"], b + 1)
                    for t in range(BT):
                        last = V.tensor_tensor(on[:, t, :].rearrange("p (h v) -> p h v", v=DH), ct[:, t, :, 0:DH],
                                               rden[:, t, :].unsqueeze(2).to_broadcast([P, H, DH]), ALU.mult)
                    last.then_inc(s["on"], 1)
                b = (slot - 23) // 8
                if k == 7 and 0 <= b < B:
                    dve.wait_ge(s["y"], b + 1)
                    dve.wait_ge(s["xb"], 1)
                    if b >= 2:
                        dve.wait_ge(s[f"st{b % 2}"], 16 * (b // 2))
                    V.tensor_tensor(ysb[:, b % 2, :, :], psM[:, 0:S].rearrange("p (t d) -> p t d", t=BT),
                                    x_sb[:, BT * b:BT * (b + 1), :], ALU.add).then_inc(s["fin"], 1)

        @block.gpsimd
        def _(pool):
            V = nc.gpsimd
            V.memset(lat[L:L + 1, :, :], 1.0).then_inc(s["latone"], 1)
            for c in range(NC):
                for t, nm in enumerate(("q", "k")):
                    pool.wait_ge(s["hi_" + nm], c + 1)
                    if c >= 1:
                        pool.wait_ge(s["lo_" + nm], c)
                        pool.wait_ge(s["mid_" + nm], c)
                    V.tensor_tensor(r32[:, t, :], q32[:, t, :], parts[:, t, 0, :], ALU.subtract).then_inc(s["r_" + nm], 1)
                    pool.wait_ge(s["mid_" + nm], c + 1)
                    V.tensor_tensor(parts[:, t, 2, :], r32[:, t, :], parts[:, t, 1, :], ALU.subtract).then_inc(s["lo_" + nm], 1)
            for c in range(NC):
                pool.wait_ge(s["ff_ev"], 2 * c + 2)
                if c >= 1:
                    pool.wait_ge(s["n2"], c)
                fc = fqT[:, :, c * CH:(c + 1) * CH]
                V.tensor_tensor(sq[:, :, :], fc, fc, ALU.mult).then_inc(s["sq"], 1)
            pool.wait_ge(s["w2"], NW2)
            pool.wait_ge(s["xn"], NC)
            V.tensor_tensor(x_sb[:, :, :], x_sb[:, :, :], bo_sb[:, :].unsqueeze(1).to_broadcast([P, NT, D]), ALU.add)\
                .then_inc(s["xb"], 1)
            pool.wait_ge(s["rn"], 1)
            for slot in range(NSLOT):
                k = slot % 8
                b = slot // 8 - 1
                if k in (3, 4) and 0 <= b < B:
                    t = k - 3
                    pool.wait_ge(s["t4"], 2 * b + t + 1)
                    pool.wait_ge(s["fs_ev"], 2 * b + t + 1)
                    if b >= 1:
                        pool.wait_ge(s["es"], b)
                        pool.wait_ge(s["fd"], b)
                    n = BT * b + t
                    gs = slice(G * t, G * (t + 1))
                    V.tensor_tensor(z_sb[:, gs, NK:KP], top8[:, gs, 0:TOP],
                                    rn[:, n, :].unsqueeze(2).to_broadcast([P, G, TOP]), ALU.mult)
                    V.tensor_tensor(z_sb[:, gs, 0:NK], s_sb[:, gs, 0:NK],
                                    rn[:, n, :].unsqueeze(2).to_broadcast([P, G, NK]), ALU.mult).then_inc(s["z"], 1)
                if k in (6, 7) and 0 <= b < B:
                    t = k - 6
                    pool.wait_ge(s["fa"], b + 1)
                    pool.wait_ge(s["es"], b + 1)
                    if b >= 1:
                        pool.wait_ge(s["wx"], b)
                    es = r_sb[:, G * t:G * (t + 1), 0:NK].rearrange("p (h a) k -> p h a k", a=2)
                    V.tensor_tensor(prod[:, t, :, :, :],
                                    es[:, :, 1, :].unsqueeze(2).to_broadcast([P, FH, TOP, NK]),
                                    a0[:, FH * t:FH * (t + 1), :].unsqueeze(3).to_broadcast([P, FH, TOP, NK]),
                                    ALU.mult).then_inc(s["pr"], 1)


NAMES = ["L0_attn_x", "L0_attn_Wq", "L0_attn_bq", "L0_attn_Wl", "L0_attn_bl", "L0_attn_Wk", "L0_attn_bk",
         "L0_attn_Wv", "L0_attn_bv", "L0_attn_Wo", "L0_attn_bo", "L0_ffn_Wq", "L0_ffn_bq", "L0_ffn_bn_gamma",
         "L0_ffn_bn_beta", "L0_ffn_sub_key0", "L0_ffn_sub_key1", "L0_ffn_expert_down", "L0_ffn_expert_up"]


def kernel(**inputs):
    import concourse.bacc as bacc
    from concourse.bass_utils import run_bass_kernel_spmd

    nc = bacc.Bacc("TRN2", target_bir_lowering=False, num_devices=1)
    arrays, args = {}, []
    for name in NAMES:
        a = np.ascontiguousarray(inputs[name])
        arrays[name] = a
        args.append(nc.dram_tensor(name, a.shape, mybir.dt.from_np(a.dtype), kind="ExternalInput").ap())
    arrays["const"] = constants()
    args.append(nc.dram_tensor("const", (P, C_END), F32, kind="ExternalInput").ap())
    shape = inputs["L0_attn_x"].shape
    args.append(nc.dram_tensor("qk_parts", (2, 3, P, shape[0] * shape[1]), BF16, kind="Internal").ap())
    args.append(nc.dram_tensor("out", shape, F32, kind="ExternalOutput").ap())
    program(nc, *args)
    return run_bass_kernel_spmd(nc, [arrays], core_ids=[0]).results[0]["out"]
```

```python
from contextlib import ExitStack

import numpy as np

import concourse.bass as bass
from concourse import mybir

F32 = mybir.dt.float32
BF16 = mybir.dt.bfloat16
ALU = mybir.AluOpType
ACT = mybir.ActivationFunctionType
AX = mybir.AxisListType.X

P = 128
NEG = -1.0e20

C_ID, C_SEL, C_AVG, C_GRP = 0, 128, 164, 292
C_END = 300


def constants():
    c = np.zeros((P, C_END), np.float32)
    p = np.arange(P)
    c[p, C_ID + p] = 1.0
    for col in range(4):
        for r in range(9):
            c[32 * col + r, C_SEL + 18 * (col % 2) + 9 * (col // 2) + r] = 1.0
    c[:, C_AVG:C_AVG + P] = (p[:, None] % 32 == p[None, :] % 32) / 8.0
    c[p, C_GRP + p // 16] = 1.0
    return c


def program(nc, x, Wq, bq, Wl, bl, Wk, bk, Wv, bv, Wo, bo,
            fWq, fbq, gamma, beta, key0, key1, down, up, const, scratch, out):
    B, S, D = x.shape
    T = B * S
    NT = T // P
    CH = 512
    NC = T // CH
    TC = CH // P
    BT = S // P
    L = Wl.shape[1]
    H, DH = 16, 8
    NPAIR = H // 2
    SCALE = float(DH) ** -0.5
    VC = DH + 1
    FH, FQ = 8, 32
    G = 2 * FH
    NK = 32
    TOP = 4
    KP = NK + TOP
    E = down.shape[0]
    TERMS = 6
    ROWS = TERMS * DH
    PART_OF = ((0, 0, 0, 1, 1, 2), (0, 1, 2, 0, 1, 0))
    RING = 4
    LAG = 11
    LN_EPS, BN_EPS, NORM_EPS = 1e-5, 1e-5, 1e-12

    xt = x.rearrange("b (n p) d -> p (b n) d", p=P)
    ot = out.rearrange("b (n p) d -> p (b n) d", p=P)

    ctx = ExitStack()
    with ctx:
        def sb(name, shape, dt=F32):
            return ctx.enter_context(nc.sbuf_tensor(name, shape, dt))

        def sem(name):
            return ctx.enter_context(nc.semaphore(name))

        cst = sb("cst", [P, C_END])
        ident = cst[:, C_ID:C_ID + P]
        sel = cst[:, C_SEL:C_SEL + 36]
        avg = cst[:, C_AVG:C_AVG + P]
        grp = cst[:, C_GRP:C_GRP + 8]
        ident_b = sb("ident_b", [P, P], BF16)
        wq_sb = sb("wq_sb", [P, D]); wl_sb = sb("wl_sb", [P, L]); wk_sb = sb("wk_sb", [L, D])
        wv_sb = sb("wv_sb", [L + 1, D]); wo_sb = sb("wo_sb", [P, D])
        fwq_sb = sb("fwq_sb", [P, 2 * P]); down_sb = sb("down_sb", [P, D]); up_sb = sb("up_sb", [P, D])
        downT = sb("downT", [P, E])
        bo_sb = sb("bo_sb", [P, D])
        vecs = sb("vecs", [P, 8])
        keys = sb("keys", [NK, 2, 16])
        keys_sq = sb("keys_sq", [NK, 2, 16])
        keys_n = sb("keys_n", [NK, 2, 3])
        keys_rep = sb("keys_rep", [NK, 4, 2, 16])
        kblk = sb("kblk", [P, 8, NK])
        x_sb = sb("x_sb", [P, NT, D])
        xnT = sb("xnT", [P, T])
        gT = xnT
        st6 = sb("st6", [P, NT, 6]); mv = sb("mv", [P, NT, 2])
        ve = sb("ve", [P, NT]); sd = sb("sd", [P, NT]); rs = sb("rs", [P, NT])
        vhat = sb("vhat", [P, NT * H * VC + 32])
        parts = sb("parts", [P, 2, 2, 3, CH], BF16)
        fst = sb("fst", [P, 2, NC, 6]); fmv = sb("fmv", [P, 2, 2])
        bnv = sb("bnv", [P, 16])
        fqT = sb("fqT", [P, 2, T])
        rn_t = sb("rn_t", [P, NT, G]); rn = sb("rn", [P, NT, G])
        QS = sb("QS", [P, RING, 2, NPAIR, S], BF16)
        KS = sb("KS", [P, RING, NPAIR, S], BF16)
        negm = sb("negm", [P, 2, 2, BT, NPAIR])
        mpart = sb("mpart", [P, BT, 2, 2, NPAIR], BF16)
        mT = sb("mT", [2 * H, S], BF16)
        Eb = sb("Eb", [P, 4, 2 * BT * S])
        xn_sb = Eb[:, 0, :].rearrange("p (a t d) -> p a t d", a=2, t=TC)
        sq = Eb[:, 1, :].rearrange("p (r n) -> p r n", r=2)
        q32 = Eb[:, 2, :].rearrange("p (r n) -> p r n", r=2)
        r32 = Eb[:, 3, :].rearrange("p (r n) -> p r n", r=2)
        Osb = sb("Osb", [P, 4, S])
        lat = Osb[0:L + 1, :, :].rearrange("p g n -> p (g n)").rearrange("p (a n) -> p a n", a=2)
        rden = sb("rden", [P, BT * H]); on = sb("on", [P, BT, D]); onT = sb("onT", [P, S])
        ysb = sb("ysb", [P, 2, BT, D])
        NH = BT * FH
        s_sb = sb("s_sb", [P, NH, 2, KP]); r_sb = sb("r_sb", [P, NH, KP])
        top8 = sb("top8", [P, NH, 2, 8]); top4 = sb("top4", [P, NH, 8])
        ZW = NK + 3 * TOP
        z_sb = sb("z_sb", [P, NH, ZW])
        den = sb("den", [P, NH, 2]); dinv = sb("dinv", [P, NH, 2])
        cmp = sb("cmp", [P, NH, TOP, TOP]); cm2 = sb("cm2", [P, NH, TOP, 2])
        ties = sb("ties", [P, NH, 6]); rank = sb("rank", [P, 4, NH, TOP])
        p0 = sb("p0", [P, NH, TOP]); p0s = sb("p0s", [P, NH, 2]); p0r = sb("p0r", [P, 3, NH])
        dd = sb("dd", [P, NH]); a0 = sb("a0", [P, NH, TOP])
        prod = sb("prod", [P, BT, FH, TOP, NK])
        wgT = sb("wgT", [P, S])

        bank = [ctx.enter_context(nc.psum_tensor(f"bank{i}", [P, 512], F32)) for i in range(4)]
        SJ = [ctx.enter_context(nc.psum_tensor(f"SJ{i}", [P, 1024], F32)) for i in range(2)]
        SI = [bank[0][:, :], bank[1][:, :]]
        psO, psM = bank[2][:, :], bank[3][:, :]
        psF = SI
        psX = [psO, SJ[1][:, 512:1024]]
        psQ, psK, psV, psL = SJ[0][:, 0:512], SJ[0][:, 512:1024], SJ[1][:, 0:512], psM
        psN = psO
        psG = [SJ[1][:, 0:512], SJ[1][:, 512:1024]]

        names = ("w0 w w2 stats aggr var std rstd xn xT xnT q q_ev l l_ev k k_ev v v_ev f f_ev f_st "
                 "hi_q hi_k r_q r_k mid_q mid_k lo_q lo_k spill0 spill1 kn1 kn2 kn3 kn4 kn5 krep kmm kblk dT downT "
                 "bn ba bb bc bd g g_ev ff sq n2 n2s n2c rn bb1 latone vone kone qzero pad identb "
                 "si mx mh ms mt mt_ev mrow sj ex pv o_ev ct rd on onp onT y fin st0 st1 "
                 "fs fs_ev t8 t4 mr z ze es fd fe cmp c2 tie rk sel p0 ps p1 p2 dd fa rest pr wt wg xb").split()
        s = {n: sem("s_" + n) for n in names}
        s_x = [sem(f"s_x{c}") for c in range(NC)]
        s_load = [sem(f"s_load{i}") for i in range(RING)]

        block = ctx.enter_context(nc.Block())
        NSLOT = NPAIR * B + LAG + 6

        def col(v):
            return v.rearrange("(p a) -> p a", a=1)

        def four(v):
            return col(v).unsqueeze(0).to_broadcast([4, FQ, 1])

        W0LOADS = [(cst[:, :], const), (fwq_sb[:, :], fWq)]
        WLOADS = [(wl_sb[:, :], Wl), (wq_sb[:, :], Wq), (wk_sb[:, :], Wk),
                  (vecs[0:L, 6:7], col(bl)), (vecs[:, 0:1], col(bq)), (vecs[:, 1:2], col(bk)),
                  (wv_sb[0:L, :], Wv), (wv_sb[L:L + 1, :], bv.rearrange("(a n) -> a n", a=1))]
        W2LOADS = [(vecs[:, 4:5], col(fbq[0:P])), (vecs[:, 5:6], col(fbq[P:2 * P])),
                   (vecs[:, 2:3], four(gamma)), (vecs[:, 3:4], four(beta)),
                   (wo_sb[:, :], Wo), (down_sb[:, :], down), (up_sb[:, :], up),
                   (keys[:, 0, :], key0), (keys[:, 1, :], key1),
                   (bo_sb[:, :], bo.rearrange("(a n) -> a n", a=1).to_broadcast([P, D]))]
        NW0, NW, NW2 = (16 * len(w) for w in (W0LOADS, WLOADS, W2LOADS))
        NSPILL = 2 * TERMS
        NLOAD = 4

        @block.sync
        def _(sp):
            for c in range(NC):
                sp.dma_start(x_sb[:, TC * c:TC * (c + 1), :], xt[:, TC * c:TC * (c + 1), :]).then_inc(s_x[c], 16)
                if c == 1:
                    for dst, src in W0LOADS:
                        sp.dma_start(dst, src).then_inc(s["w0"], 16)
                if c == 3:
                    for dst, src in WLOADS:
                        sp.dma_start(dst, src).then_inc(s["w"], 16)
            for dst, src in W2LOADS:
                sp.dma_start(dst, src).then_inc(s["w2"], 16)

            def spill(c):
                for t in range(2):
                    sp.wait_ge(s["lo_q" if t == 0 else "lo_k"], c + 1)
                    for term, part in enumerate(PART_OF[t]):
                        sp.dma_start(scratch[t, c, :, term],
                                     parts[:, c % 2, t, part, :]).then_inc(s[f"spill{c % 2}"], 16)

            def store(b):
                sp.wait_ge(s["fin"], b + 1)
                sp.dma_start(ot[:, BT * b:BT * (b + 1), :], ysb[:, b % 2, :, :]).then_inc(s[f"st{b % 2}"], 16)

            def load(b):
                c, o = b // 2, (b % 2) * S
                sp.wait_ge(s[f"spill{c % 2}"], 16 * NSPILL * (c // 2 + 1))
                if b >= RING:
                    sp.wait_ge(s["sj"], NPAIR * (b - RING + 1))
                for e in range(2):
                    for t, dst in ((0, QS[:, b % RING, e]), (1, KS[:, b % RING])):
                        src = scratch[t, c, NPAIR * e:NPAIR * (e + 1)].rearrange("r a d n -> (a d) r n")
                        sp.dma_start(dst[64 * e:64 * e + ROWS], src[:, :, o:o + S]).then_inc(s_load[b % RING], 16)

            def max_rows(b):
                sp.wait_ge(s["mt_ev"], b + 1)
                for e in range(2):
                    for part in range(2):
                        src = (e * 2 + part) * NPAIR
                        r0 = 64 * e + ROWS + part
                        sp.dma_start(QS[r0:r0 + 1, b % RING, e, :, :], mT[src:src + NPAIR, :]).then_inc(s["mrow"], 16)

            sp.wait_ge(s["kone"], 1)
            sp.wait_ge(s["qzero"], 1)
            spill(0)
            load(0)
            load(1)
            for c in range(1, NC):
                spill(c)
                if c == 1:
                    load(2)
                    load(3)
            for it in range(1, B + 4):
                if it <= B:
                    max_rows(it - 1)
                if RING <= it + 2 < B:
                    load(it + 2)
                if it >= 4:
                    store(it - 4)
            for e in range(2):
                sp.wait_ge(s[f"st{e}"], 16 * B // 2)

        @block.scalar
        def _(act):
            A = nc.scalar.activation

            def latent(c):
                act.wait_ge(s["l"], c + 1)
                if c == 0:
                    act.wait_ge(s["w"], NW)
                A(lat[0:L, c % 2, :], psL[0:L, :], ACT.Identity, bias=vecs[0:L, 6:7]).then_inc(s["l_ev"], 1)

            def qkv(c):
                act.wait_ge(s["v"], c + 1)
                act.wait_ge(s["vone"], 1)
                A(vhat[:, TC * c * H * VC:TC * (c + 1) * H * VC].rearrange("p (n v) -> p n v", v=VC)[:, :, 0:DH],
                  psV.rearrange("p (n v) -> p n v", v=DH), ACT.Copy).then_inc(s["v_ev"], 1)
                if c >= 2:
                    act.wait_ge(s[f"spill{c % 2}"], 16 * NSPILL * (c // 2))
                for t, nm in enumerate(("q", "k")):
                    act.wait_ge(s[nm + "_ev"], c + 1)
                    A(parts[:, c % 2, t, 0, :], q32[:, t, :], ACT.Copy).then_inc(s["hi_" + nm], 1)
                for t, nm in enumerate(("q", "k")):
                    act.wait_ge(s["r_" + nm], c + 1)
                    A(parts[:, c % 2, t, 1, :], r32[:, t, :], ACT.Copy).then_inc(s["mid_" + nm], 1)

            for c in range(NC + 2):
                if c < NC:
                    act.wait_ge(s["var"], c + 1)
                    A(sd[:, TC * c:TC * (c + 1)], ve[:, TC * c:TC * (c + 1)], ACT.Sqrt).then_inc(s["std"], 1)
                if 1 <= c <= NC:
                    act.wait_ge(s["xT"], c)
                    A(xnT[:, (c - 1) * CH:c * CH], psX[(c - 1) % 2], ACT.Copy).then_inc(s["xnT"], 1)
                if c == 2:
                    latent(0)
                if c == 3:
                    qkv(0)
                if c >= 2:
                    for r in range(2):
                        act.wait_ge(s["f"], 2 * (c - 2) + r + 1)
                        A(fqT[:, r, (c - 2) * CH:(c - 1) * CH], psF[r], ACT.Copy).then_inc(s["f_ev"], 1)
            act.wait_ge(s["kn2"], 1)
            A(keys_n[:, :, 1], keys_n[:, :, 0], ACT.Sqrt).then_inc(s["kn3"], 1)
            act.wait_ge(s["bc"], 1)
            A(bnv[:, 6:7], bnv[:, 5:6], ACT.Sqrt).then_inc(s["bd"], 1)

            for slot in range(NSLOT):
                k = slot % 8
                if 1 <= slot < NC:
                    latent(slot)
                if slot < NC:
                    act.wait_ge(s["ff"], slot + 1)
                    if slot >= 1:
                        act.wait_ge(s["n2"], slot)
                    A(sq[:, :, :], fqT[:, :, slot * CH:(slot + 1) * CH], ACT.Square).then_inc(s["sq"], 1)
                if 1 <= slot < NC:
                    qkv(slot)
                if slot == NC:
                    act.wait_ge(s["n2"], NC)
                    A(rn_t[:, :, :], psN.rearrange("p (n g) -> p n g", g=G), ACT.Sqrt).then_inc(s["n2s"], 1)
                b = slot // 8 - 1
                if k == 1 and 0 <= b < B:
                    act.wait_ge(s["mt"], b + 1)
                    if b >= 1:
                        act.wait_ge(s["mrow"], 64 * b)
                    A(mT[:, :], psM[0:2 * H, 0:S], ACT.Copy).then_inc(s["mt_ev"], 1)
                if k in (2, 3) and 0 <= b < B:
                    t = k - 2
                    act.wait_ge(s["fs"], 2 * b + t + 1)
                    act.wait_ge(s["pad"], 1)
                    if b >= 1:
                        act.wait_ge(s["mr"], 2 * b)
                        act.wait_ge(s["sel"], b)
                    A(s_sb[:, FH * t:FH * (t + 1), :, 0:NK].rearrange("p h a k -> p (h a) k"),
                      psM.rearrange("p (g k) -> p g k", k=NK), ACT.Copy).then_inc(s["fs_ev"], 1)
                m = slot - LAG - 4
                if m >= 0 and m % 2 == 0 and m // 2 < 4 * B:
                    g = m // 2
                    act.wait_ge(s["pv"], g + 1)
                    if g >= 4:
                        act.wait_ge(s["ct"], g // 4)
                    A(Osb[:, g % 4, :], psO[:, (g % 2) * S:(g % 2 + 1) * S], ACT.Copy).then_inc(s["o_ev"], 1)
                ba = (slot - LAG - 12) // 8
                if k == 7 and 0 <= ba < B:
                    act.wait_ge(s["onp"], ba + 1)
                    if ba >= 1:
                        act.wait_ge(s["y"], ba)
                    A(onT[:, :], psM[:, 0:S], ACT.Copy).then_inc(s["onT"], 1)
                n = slot - LAG
                if 0 <= n < NPAIR * B:
                    act.wait_ge(s["sj"], n + 1)
                    if n >= 4:
                        act.wait_ge(s["pv"], (n - 4) // 2 + 1)
                    elif n == 0:
                        act.wait_ge(s["lo_q"], NC)
                        act.wait_ge(s["lo_k"], NC)
                    A(Eb[:, n % 4, :], SJ[n % 2][:, :], ACT.Exp).then_inc(s["ex"], 1)
                if slot in (NC, NC + 1):
                    for c in range(4 * (slot - NC), 4 * (slot - NC + 1)):
                        act.wait_ge(s["g"], c + 1)
                        A(gT[:, c * CH:(c + 1) * CH], psG[c % 2], ACT.Gelu).then_inc(s["g_ev"], 1)
                if k == 5 and 0 <= b < B:
                    act.wait_ge(s["z"], b + 1)
                    A(z_sb[:, :, :], z_sb[:, :, :], ACT.Exp).then_inc(s["ze"], 1)

        @block.tensor
        def _(pe):
            mm = nc.tensor.matmul

            def qkv_latent(c):
                xc = xnT[:, c * CH:(c + 1) * CH]
                if c >= 1:
                    pe.wait_ge(s["l_ev"], c)
                    pe.wait_ge(s["q_ev"], c)
                mm(psL[0:L, :], wl_sb[:, :], xc, start=True, stop=True).then_inc(s["l"], 1)
                mm(psQ, wq_sb[:, :], xc, start=True, stop=True).then_inc(s["q"], 1)

            def qkv_rest(c):
                pe.wait_ge(s["l_ev"], c + 1)
                if c >= 1:
                    pe.wait_ge(s["v_ev"], c)
                    pe.wait_ge(s["k_ev"], c)
                mm(psK, wk_sb[:, :], lat[0:L, c % 2, :], start=True, stop=True).then_inc(s["k"], 1)
                for t in range(TC):
                    last = mm(psV[:, t * P:(t + 1) * P], lat[:, c % 2, t * P:(t + 1) * P], wv_sb[:, :], start=True, stop=True)
                last.then_inc(s["v"], 1)

            pe.wait_ge(s["w0"], NW0)
            for c in range(NC + 1):
                if c < NC:
                    pe.wait_ge(s["xn"], c + 1)
                    if c >= 2:
                        pe.wait_ge(s["xnT"], c - 1)
                    for t in range(TC):
                        last = mm(psX[c % 2][:, t * P:(t + 1) * P], xn_sb[:, c % 2, t, :], ident, start=True, stop=True)
                    last.then_inc(s["xT"], 1)
                if c >= 1:
                    pe.wait_ge(s["xnT"], c)
                    if c == 1:
                        pe.wait_ge(s["w"], NW)
                        pe.wait_ge(s["latone"], 1)
                        qkv_latent(0)
                    for r in range(2):
                        if c >= 2:
                            pe.wait_ge(s["f_ev"], 2 * (c - 2) + r + 1)
                        mm(psF[r], fwq_sb[:, r * P:(r + 1) * P], xnT[:, (c - 1) * CH:c * CH],
                           start=True, stop=True).then_inc(s["f"], 1)
                    if c == 2:
                        qkv_rest(0)
            pe.wait_ge(s["krep"], 1)
            pe.wait_ge(s["xnT"], NC)
            mm(psX[1][:, 0:NK], keys_rep[:, :, :, :].rearrange("k h a d -> k (h a d)"), cst[0:NK, 0:NK],
               start=True, stop=True).then_inc(s["kmm"], 1)
            mm(psX[0][:, 0:E], down_sb[:, :], ident, start=True, stop=True).then_inc(s["dT"], 1)
            pe.wait_ge(s["ba"], 1)
            pe.wait_ge(s["downT"], 1)
            for r in range(2):
                last = mm(psX[0][:, 0:1], avg, bnv[:, r:r + 1], start=(r == 0), stop=(r == 1))
            last.then_inc(s["ba"], 1)
            pe.wait_ge(s["bb"], 1)
            for r in range(2):
                last = mm(psX[0][:, 2:3], avg, bnv[:, 2 + r:3 + r], start=(r == 0), stop=(r == 1))
            last.then_inc(s["bb"], 1)
            pe.wait_ge(s["bc"], 1)
            pe.wait_ge(s["identb"], 1)

            def si(n):
                b, pr = n // NPAIR, n % NPAIR
                if pr == 0:
                    pe.wait_ge(s_load[b % RING], 16 * NLOAD * (b // RING + 1))
                for e in range(2):
                    if n >= 1:
                        pe.wait_ge(s["mx"], 2 * (n - 1) + e + 1)
                    else:
                        pe.wait_ge(s["f_ev"], 2 * NC)
                    r = slice(64 * e, 64 * e + ROWS)
                    for t in range(BT):
                        last = mm(SI[e][:, t * S:(t + 1) * S], QS[r, b % RING, e, pr, t * P:(t + 1) * P],
                                  KS[r, b % RING, pr, :], start=True, stop=True)
                    last.then_inc(s["si"], 1)

            def norms(c):
                pe.wait_ge(s["sq"], c + 1)
                for t in range(TC):
                    for r in range(2):
                        o = (c * TC + t) * G + 8 * r
                        last = mm(psN[:, o:o + 8], sq[:, r, t * P:(t + 1) * P], grp, start=True, stop=True)
                last.then_inc(s["n2"], 1)

            for slot in range(NSLOT):
                k = slot % 8
                if 1 <= slot < NC:
                    qkv_latent(slot)
                if slot < NPAIR * B:
                    si(slot)
                if 1 <= slot <= NC:
                    norms(slot - 1)
                if 1 <= slot < NC:
                    qkv_rest(slot)
                n = slot - LAG
                if 0 <= n < NPAIR * B:
                    b, pr = n // NPAIR, n % NPAIR
                    if pr == 0:
                        pe.wait_ge(s["mrow"], 64 * (b + 1))
                    if n >= 2:
                        pe.wait_ge(s["ex"], n - 1)
                    else:
                        pe.wait_ge(s["k_ev"], NC)
                        pe.wait_ge(s["g_ev"], NC)
                    for e in range(2):
                        for t in range(BT):
                            last = mm(SJ[n % 2][:, (e * BT + t) * S:(e * BT + t + 1) * S],
                                      KS[:, b % RING, pr, t * P:(t + 1) * P],
                                      QS[:, b % RING, e, pr, :], start=True, stop=True)
                    last.then_inc(s["sj"], 1)
                m = slot - LAG - 3
                if m >= 0 and m % 2 == 0 and m // 2 < 4 * B:
                    g = m // 2
                    b = g // 4
                    pe.wait_ge(s["ex"], 2 * g + 2)
                    if g >= 1:
                        pe.wait_ge(s["o_ev"], g)
                    else:
                        pe.wait_ge(s["n2s"], 1)
                        pe.wait_ge(s["v_ev"], NC)
                    for t in range(BT):
                        for c in range(4):
                            h = 2 * (g % 4) + c // 2 + NPAIR * (c % 2)
                            v0 = ((BT * b + t) * H + h) * VC
                            e0 = ((c % 2) * BT + t) * S
                            last = mm(psO[32 * c:32 * c + 32, (g % 2) * S:(g % 2 + 1) * S], vhat[:, v0:v0 + 32],
                                      Eb[:, (2 * g + c // 2) % 4, e0:e0 + S], start=(t == 0), stop=(t == BT - 1),
                                      tile_position=(0, 32 * c), skip_group_check=True)
                    last.then_inc(s["pv"], 1)
                b = slot // 8 - 1
                if k == 0 and 0 <= b < B:
                    pe.wait_ge(s["ms"], b + 1)
                    if b >= 2:
                        pe.wait_ge(s["fin"], b - 1)
                    for t in range(BT):
                        last = mm(psM[0:2 * H, t * P:(t + 1) * P], mpart[:, t, :, :, :].rearrange("p e a r -> p (e a r)"),
                                  ident_b[:, :], start=True, stop=True)
                    last.then_inc(s["mt"], 1)
                if k in (1, 2) and 0 <= b < B:
                    t = k - 1
                    if t == 0:
                        pe.wait_ge(s["mt_ev"], b + 1)
                    else:
                        pe.wait_ge(s["fs_ev"], 2 * b + 1)
                    tok = (BT * b + t) * P
                    for r in range(2):
                        last = mm(psM[:, 256 * r:256 * (r + 1)], fqT[:, r, tok:tok + P],
                                  kblk[:, :, :].rearrange("p g k -> p (g k)"), start=True, stop=True)
                    last.then_inc(s["fs"], 1)
                if slot in (NC, NC + 1):
                    for c in range(4 * (slot - NC), 4 * (slot - NC + 1)):
                        if c >= 2:
                            pe.wait_ge(s["g_ev"], c - 1)
                        else:
                            pe.wait_ge(s["v_ev"], NC)
                            pe.wait_ge(s["kblk"], 1)
                        mm(psG[c % 2], downT[:, :], xnT[:, c * CH:(c + 1) * CH], start=True, stop=True).then_inc(s["g"], 1)
                b = (slot - LAG - 8) // 8
                if k == 3 and 0 <= b < B:
                    pe.wait_ge(s["pr"], 4 * (b + 1))
                    if b + 1 < B:
                        pe.wait_ge(s["fs_ev"], 2 * (b + 2))
                    else:
                        pe.wait_ge(s["fin"], b)
                    for t in range(BT):
                        for h in range(FH // 2):
                            last = mm(psM[:, t * P:(t + 1) * P], prod[:, t, h, :, :].rearrange("p i j -> p (i j)"), ident,
                                      start=(h == 0), stop=(h == FH // 2 - 1))
                    last.then_inc(s["wt"], 1)
                b = (slot - LAG - 10) // 8
                if k == 5 and 0 <= b < B:
                    pe.wait_ge(s["wg"], b + 1)
                    pe.wait_ge(s["o_ev"], 4 * (b + 1))
                    for t in range(BT):
                        for g in range(4):
                            ct = psM[:, t * H * VC:(t + 1) * H * VC].rearrange("p (e n) -> p e n", e=2)
                            last = mm(ct[:, :, 2 * g * VC:2 * (g + 1) * VC], Osb[:, g, t * P:(t + 1) * P],
                                      sel, start=True, stop=True)
                    last.then_inc(s["ct"], 1)
                b = (slot - LAG - 11) // 8
                if k == 6 and 0 <= b < B:
                    pe.wait_ge(s["on"], b + 1)
                    for t in range(BT):
                        last = mm(psM[:, t * P:(t + 1) * P], on[:, t, :], ident, start=True, stop=True)
                    last.then_inc(s["onp"], 1)
                b = (slot - LAG - 12) // 8
                if k == 7 and 0 <= b < B:
                    pe.wait_ge(s["onT"], b + 1)
                    for t in range(BT):
                        mm(psM[:, t * D:(t + 1) * D], onT[:, t * P:(t + 1) * P], wo_sb[:, :], start=True, stop=False)
                        last = mm(psM[:, t * D:(t + 1) * D], wgT[:, t * P:(t + 1) * P], up_sb[:, :], start=False, stop=True)
                    last.then_inc(s["y"], 1)

        @block.vector
        def _(dve):
            V = nc.vector
            step = [0]

            def chain(i):
                step[0] += 1
                i.then_inc(s["bb1"], 1)
                dve.wait_ge(s["bb1"], step[0])

            def q_ev(c):
                dve.wait_ge(s["q"], c + 1)
                if c == 0:
                    dve.wait_ge(s["w"], NW)
                if c >= 1:
                    dve.wait_ge(s["r_q"], c)
                    dve.wait_ge(s["hi_q"], c)
                V.tensor_scalar(q32[:, 0, :], psQ, vecs[:, 0:1], SCALE, ALU.add, ALU.mult).then_inc(s["q_ev"], 1)

            def k_ev(c):
                dve.wait_ge(s["k"], c + 1)
                if c >= 1:
                    dve.wait_ge(s["r_k"], c)
                    dve.wait_ge(s["hi_k"], c)
                V.tensor_scalar(q32[:, 1, :], psK, vecs[:, 1:2], None, ALU.add).then_inc(s["k_ev"], 1)

            def lo_k(c):
                dve.wait_ge(s["mid_k"], c + 1)
                V.tensor_tensor(parts[:, c % 2, 1, 2, :], r32[:, 1, :], parts[:, c % 2, 1, 1, :], ALU.subtract)\
                    .then_inc(s["lo_k"], 1)

            for c in range(NC + 3):
                if c < NC:
                    dve.wait_ge(s_x[c], 16)
                    tiles = range(TC * c, TC * (c + 1))
                    for n in tiles:
                        last = V.bn_stats(st6[:, n, :], x_sb[:, n, :])
                    last.then_inc(s["stats"], 1)
                    dve.wait_ge(s["stats"], c + 1)
                    for n in tiles:
                        last = V.bn_aggr(mv[:, n, :], st6[:, n, :])
                    last.then_inc(s["aggr"], 1)
                    dve.wait_ge(s["aggr"], c + 1)
                    V.tensor_scalar(ve[:, TC * c:TC * (c + 1)], mv[:, TC * c:TC * (c + 1), 1], LN_EPS, None, ALU.add)\
                        .then_inc(s["var"], 1)
                if c == 3:
                    q_ev(0)
                    k_ev(0)
                if c >= 3:
                    for r in range(2):
                        dve.wait_ge(s["f_ev"], 2 * (c - 3) + r + 1)
                        V.bn_stats(fst[:, r, c - 3, :], fqT[:, r, (c - 3) * CH:(c - 2) * CH]).then_inc(s["f_st"], 1)
                if c == 4:
                    lo_k(0)
                if c < NC:
                    dve.wait_ge(s["std"], c + 1)
                    V.reciprocal(rs[:, TC * c:TC * (c + 1)], sd[:, TC * c:TC * (c + 1)]).then_inc(s["rstd"], 1)
                    dve.wait_ge(s["rstd"], c + 1)
                    if c >= 2:
                        dve.wait_ge(s["xT"], c - 1)
                    for n in tiles:
                        last = V.tensor_scalar(xn_sb[:, c % 2, n % TC, :], x_sb[:, n, :], mv[:, n, 0:1], rs[:, n:n + 1],
                                               ALU.subtract, ALU.mult)
                    last.then_inc(s["xn"], 1)
                if c == NC - 1:
                    dve.wait_ge(s["w0"], NW0)
                    V.tensor_copy(ident_b[:, :], ident).then_inc(s["identb"], 1)
                    dve.wait_ge(s["w2"], NW2)
                    V.tensor_tensor(keys_sq[:, :, :], keys[:, :, :], keys[:, :, :], ALU.mult).then_inc(s["kn1"], 1)
                    dve.wait_ge(s["kn1"], 1)
                    V.tensor_reduce(keys_n[:, :, 0], keys_sq[:, :, :], axis=AX, op=ALU.add).then_inc(s["kn2"], 1)
            dve.wait_ge(s["kn3"], 1)
            V.tensor_scalar(keys_n[:, :, 2], keys_n[:, :, 1], NORM_EPS, None, ALU.max).then_inc(s["kn4"], 1)
            dve.wait_ge(s["kn4"], 1)
            V.reciprocal(keys_n[:, :, 0], keys_n[:, :, 2]).then_inc(s["kn5"], 1)
            dve.wait_ge(s["kn5"], 1)
            for h in range(4):
                last = V.tensor_tensor(keys_rep[:, h, :, :], keys[:, :, :],
                                       keys_n[:, :, 0:1].to_broadcast([NK, 2, 16]), ALU.mult)
            last.then_inc(s["krep"], 1)
            dve.wait_ge(s["f_st"], 2 * NC)
            for r in range(2):
                last = V.bn_aggr(fmv[:, r, :], fst[:, r, :, :])
            chain(last)
            V.tensor_tensor(bnv[:, 0:2], fmv[:, :, 0], vecs[:, 4:6], ALU.add).then_inc(s["ba"], 1)
            dve.wait_ge(s["dT"], 1)
            V.tensor_copy(downT[:, :], psX[0][:, 0:E]).then_inc(s["downT"], 1)
            dve.wait_ge(s["kmm"], 1)
            V.tensor_tensor(kblk[:, :, :], psX[1][:, 0:NK].unsqueeze(1).to_broadcast([P, 8, NK]),
                            grp.unsqueeze(2).to_broadcast([P, 8, NK]), ALU.mult).then_inc(s["kblk"], 1)
            dve.wait_ge(s["ba"], 2)
            chain(V.tensor_copy(bnv[:, 4:5], psX[0][:, 0:1]))
            chain(V.tensor_scalar(bnv[:, 10:12], bnv[:, 0:2], bnv[:, 4:5], None, ALU.subtract))
            chain(V.tensor_tensor(bnv[:, 12:14], bnv[:, 10:12], bnv[:, 10:12], ALU.mult))
            V.tensor_tensor(bnv[:, 2:4], bnv[:, 12:14], fmv[:, :, 1], ALU.add).then_inc(s["bb"], 1)
            dve.wait_ge(s["bb"], 2)
            V.tensor_scalar(bnv[:, 5:6], psX[0][:, 2:3], BN_EPS, None, ALU.add).then_inc(s["bc"], 1)
            dve.wait_ge(s["bd"], 1)
            chain(V.reciprocal(bnv[:, 14:15], bnv[:, 6:7]))
            V.tensor_scalar(bnv[:, 10:12], vecs[:, 4:6], bnv[:, 4:5], None, ALU.subtract)
            chain(V.tensor_tensor(bnv[:, 7:8], bnv[:, 14:15], vecs[:, 2:3], ALU.mult))
            V.tensor_scalar(bnv[:, 8:10], bnv[:, 10:12], bnv[:, 7:8], vecs[:, 3:4], ALU.mult, ALU.add).then_inc(s["bn"], 1)
            dve.wait_ge(s["bn"], 1)

            for slot in range(NSLOT):
                k = slot % 8
                b = (slot - LAG - 9) // 8
                if k == 4 and 0 <= b < B:
                    dve.wait_ge(s["wt"], b + 1)
                    dve.wait_ge(s["g_ev"], NC)
                    if b >= 1:
                        dve.wait_ge(s["y"], b)
                    V.tensor_tensor(wgT[:, :], psM[:, 0:S], gT[:, b * S:(b + 1) * S], ALU.mult).then_inc(s["wg"], 1)
                b = (slot - LAG - 11) // 8
                if k == 6 and 0 <= b < B:
                    dve.wait_ge(s["ct"], b + 1)
                    ct = psM[:, 0:BT * H * VC].rearrange("p (h v) -> p h v", v=VC)
                    if b >= 1:
                        dve.wait_ge(s["onp"], b)
                    V.reciprocal(rden[:, :], ct[:, :, DH]).then_inc(s["rd"], 1)
                    dve.wait_ge(s["rd"], b + 1)
                    V.tensor_tensor(on[:, :, :].rearrange("p t (h v) -> p (t h) v", v=DH), ct[:, :, 0:DH],
                                    rden[:, :].unsqueeze(2).to_broadcast([P, BT * H, DH]), ALU.mult).then_inc(s["on"], 1)
                b = (slot - LAG - 13) // 8
                if k == 0 and 0 <= b < B:
                    dve.wait_ge(s["y"], b + 1)
                    dve.wait_ge(s["xb"], 1)
                    if b >= 2:
                        dve.wait_ge(s[f"st{b % 2}"], 16 * (b // 2))
                    V.tensor_tensor(ysb[:, b % 2, :, :], psM[:, 0:S].rearrange("p (t d) -> p t d", t=BT),
                                    x_sb[:, BT * b:BT * (b + 1), :], ALU.add).then_inc(s["fin"], 1)
                b = slot // 8 - 1
                if k == 0 and 0 <= b < B:
                    dve.wait_ge(s["mx"], 2 * NPAIR * (b + 1))
                    if b >= 1:
                        dve.wait_ge(s["mt"], b)
                    src = negm[:, b % 2, :, :, :].rearrange("p e t r -> p t e r")
                    V.tensor_copy(mpart[:, :, :, 0, :], src).then_inc(s["mh"], 1)
                    dve.wait_ge(s["mh"], b + 1)
                    V.tensor_tensor(mpart[:, :, :, 1, :], src, mpart[:, :, :, 0, :], ALU.subtract).then_inc(s["ms"], 1)
                if slot < NC:
                    fc = fqT[:, :, slot * CH:(slot + 1) * CH]
                    for r in range(2):
                        last = V.tensor_scalar(fc[:, r, :], fc[:, r, :], bnv[:, 7:8], bnv[:, 8 + r:9 + r], ALU.mult, ALU.add)
                    last.then_inc(s["ff"], 1)
                if 1 <= slot < NC:
                    q_ev(slot)
                if slot < NPAIR * B:
                    bb, pr = slot // NPAIR, slot % NPAIR
                    for e in range(2):
                        dve.wait_ge(s["si"], 2 * slot + e + 1)
                        V.tensor_reduce(negm[:, bb % 2, e, :, pr], SI[e].rearrange("p (t j) -> p t j", j=S),
                                        axis=AX, op=ALU.max, negate=True).then_inc(s["mx"], 1)
                if 1 <= slot < NC:
                    k_ev(slot)
                if 2 <= slot <= NC:
                    lo_k(slot - 1)
                if slot == NC:
                    dve.wait_ge(s["n2s"], 1)
                    V.tensor_scalar(rn_t[:, :, :], rn_t[:, :, :], NORM_EPS, None, ALU.max).then_inc(s["n2c"], 1)
                    dve.wait_ge(s["n2c"], 1)
                    V.reciprocal(rn[:, :, :], rn_t[:, :, :]).then_inc(s["rn"], 1)
                if k in (2, 3) and 0 <= b < B:
                    t = k - 2
                    dve.wait_ge(s["fs_ev"], 2 * b + t + 1)
                    if b >= 1:
                        dve.wait_ge(s["sel"], b)
                        dve.wait_ge(s["t4"], 2 * b)
                    for h in range(FH * t, FH * (t + 1)):
                        for a in range(2):
                            last = V.max(top8[:, h, a, :], s_sb[:, h, a, 0:NK])
                    last.then_inc(s["t8"], 1)
                if k in (4, 5) and 0 <= b < B:
                    t = k - 4
                    dve.wait_ge(s["t4"], 2 * b + t + 1)
                    if b >= 1:
                        dve.wait_ge(s["pr"], 4 * b)
                    for h in range(FH * t, FH * (t + 1)):
                        last = V.match_replace(r_sb[:, h, :], top4[:, h, :], s_sb[:, h, 1, :], NEG)
                    last.then_inc(s["mr"], 1)
                if k == 6 and 0 <= b < B:
                    dve.wait_ge(s["ze"], b + 1)
                    dve.wait_ge(s["mr"], 2 * b + 2)
                    if b >= 1:
                        dve.wait_ge(s["fa"], b)
                        dve.wait_ge(s["rest"], b)
                    V.tensor_reduce(den[:, :, :], z_sb[:, :, NK + TOP:ZW].rearrange("p h (a k) -> p h a k", a=2),
                                    axis=AX, op=ALU.add).then_inc(s["fd"], 1)
                    V.scalar_tensor_tensor(r_sb[:, :, 0:NK], r_sb[:, :, 0:NK], NEG, z_sb[:, :, 0:NK],
                                           ALU.is_equal, ALU.mult).then_inc(s["es"], 1)
                    dve.wait_ge(s["fd"], b + 1)
                    V.reciprocal(dinv[:, :, :], den[:, :, :]).then_inc(s["fe"], 1)

        @block.gpsimd
        def _(pool):
            V = nc.gpsimd
            TT = V.tensor_tensor
            V.memset(lat[L:L + 1, :, :], 1.0).then_inc(s["latone"], 1)
            pool.wait_ge(s["latone"], 1)
            V.memset(vhat[:, :], 1.0).then_inc(s["vone"], 1)
            V.memset(QS[:, :, :, :, :].rearrange("p c e r n -> p (c e r n)").bitcast(mybir.dt.uint32), 0).then_inc(s["qzero"], 1)
            V.memset(KS[:, :, :, :].rearrange("p a r n -> p (a r n)"), 1.0).then_inc(s["kone"], 1)
            V.memset(s_sb[:, :, :, NK:KP], NEG)
            V.memset(top4[:, :, TOP:8], NEG).then_inc(s["pad"], 1)

            def residues(c):
                for t, nm in enumerate(("q", "k")):
                    pool.wait_ge(s["hi_" + nm], c + 1)
                    if c >= 1:
                        pool.wait_ge(s["lo_" + nm], c)
                        pool.wait_ge(s["mid_" + nm], c)
                    TT(r32[:, t, :], q32[:, t, :], parts[:, c % 2, t, 0, :], ALU.subtract).then_inc(s["r_" + nm], 1)
                pool.wait_ge(s["mid_q"], c + 1)
                TT(parts[:, c % 2, 0, 2, :], r32[:, 0, :], parts[:, c % 2, 0, 1, :], ALU.subtract).then_inc(s["lo_q"], 1)

            residues(0)
            for slot in range(NSLOT):
                k = slot % 8
                b = slot // 8 - 1
                if 1 <= slot < NC:
                    residues(slot)
                if slot == NC:
                    pool.wait_ge(s["w2"], NW2)
                    pool.wait_ge(s["xn"], NC)
                    TT(x_sb[:, :, :], x_sb[:, :, :], bo_sb[:, :].unsqueeze(1).to_broadcast([P, NT, D]), ALU.add)\
                        .then_inc(s["xb"], 1)
                    pool.wait_ge(s["rn"], 1)
                if k in (3, 4) and 0 <= b < B:
                    t = k - 3
                    hs = slice(FH * t, FH * (t + 1))
                    pool.wait_ge(s["t8"], 2 * b + t + 1)
                    if b >= 1:
                        pool.wait_ge(s["mr"], 2 * b)
                    V.tensor_copy(top4[:, hs, 0:TOP], top8[:, hs, 1, 0:TOP]).then_inc(s["t4"], 1)
                if k == 4 and 0 <= b < B:
                    pool.wait_ge(s["fs_ev"], 2 * b + 2)
                    if b >= 1:
                        pool.wait_ge(s["es"], b)
                        pool.wait_ge(s["fd"], b)
                        pool.wait_ge(s["p0"], b)
                    rb = rn[:, BT * b:BT * (b + 1), :].rearrange("p t (h a) -> p (t h) a", a=2)

                    def per(a, n):
                        return rb[:, :, a:a + 1].to_broadcast([P, NH, n])
                    TT(z_sb[:, :, NK:NK + TOP], s_sb[:, :, 0, 0:TOP], per(0, TOP), ALU.mult)
                    TT(z_sb[:, :, NK + TOP:NK + 2 * TOP], top8[:, :, 0, 0:TOP], per(0, TOP), ALU.mult)
                    TT(z_sb[:, :, NK + 2 * TOP:ZW], top8[:, :, 1, 0:TOP], per(1, TOP), ALU.mult)
                    TT(z_sb[:, :, 0:NK], s_sb[:, :, 1, 0:NK], per(1, NK), ALU.mult).then_inc(s["z"], 1)
                    first = s_sb[:, :, 0, 0:TOP]
                    best = top8[:, :, 0, 0:TOP]
                    TT(cmp[:, :, :, :], best.unsqueeze(2).to_broadcast([P, NH, TOP, TOP]),
                       first.unsqueeze(3).to_broadcast([P, NH, TOP, TOP]), ALU.subtract).then_inc(s["cmp"], 1)
                    TT(ties[:, :, 0:3], first[:, :, 1:4], first[:, :, 0:3], ALU.subtract)
                    TT(ties[:, :, 3:5], first[:, :, 2:4], first[:, :, 0:2], ALU.subtract)
                    TT(ties[:, :, 5:6], first[:, :, 3:4], first[:, :, 0:1], ALU.subtract).then_inc(s["tie"], 1)
                    pool.wait_ge(s["cmp"], 2 * b + 1)
                    V.tensor_scalar(cmp[:, :, :, :], cmp[:, :, :, :], 0.0, None, ALU.is_gt).then_inc(s["cmp"], 1)
                    pool.wait_ge(s["tie"], 2 * b + 1)
                    V.tensor_scalar(ties[:, :, :], ties[:, :, :], 0.0, None, ALU.is_equal).then_inc(s["tie"], 1)
                    pool.wait_ge(s["cmp"], 2 * b + 2)
                    TT(cm2[:, :, :, :], cmp[:, :, :, 0:2], cmp[:, :, :, 2:4], ALU.add).then_inc(s["c2"], 1)
                    pool.wait_ge(s["c2"], b + 1)
                    TT(rank[:, 0, :, :], cm2[:, :, :, 0], cm2[:, :, :, 1], ALU.add).then_inc(s["rk"], 1)
                    pool.wait_ge(s["tie"], 2 * b + 2)
                    for i, (lo, n, at) in enumerate(((1, 3, 0), (2, 2, 3), (3, 1, 5))):
                        pool.wait_ge(s["rk"], 4 * b + i + 1)
                        TT(rank[:, 0, :, lo:TOP], rank[:, 0, :, lo:TOP], ties[:, :, at:at + n], ALU.add).then_inc(s["rk"], 1)
                    pool.wait_ge(s["rk"], 4 * b + 4)
                    V.tensor_scalar(rank[:, 1, :, :], rank[:, 0, :, :], float(TOP), None, ALU.is_lt).then_inc(s["sel"], 1)
                if k == 6 and 0 <= b < B:
                    pool.wait_ge(s["ze"], b + 1)
                    pool.wait_ge(s["sel"], b + 1)
                    TT(p0[:, :, :], rank[:, 1, :, :], z_sb[:, :, NK:NK + TOP], ALU.mult).then_inc(s["p0"], 1)
                    pool.wait_ge(s["p0"], b + 1)
                    TT(p0s[:, :, :], p0[:, :, 0:2], p0[:, :, 2:4], ALU.add).then_inc(s["ps"], 1)
                    pool.wait_ge(s["ps"], b + 1)
                    TT(p0r[:, 0, :], p0s[:, :, 0], p0s[:, :, 1], ALU.add).then_inc(s["p1"], 1)
                    pool.wait_ge(s["fe"], b + 1)
                    TT(dd[:, :], dinv[:, :, 0], dinv[:, :, 1], ALU.mult).then_inc(s["dd"], 1)
                    pool.wait_ge(s["p1"], b + 1)
                    TT(p0r[:, 1, :], den[:, :, 0], p0r[:, 0, :], ALU.subtract).then_inc(s["p2"], 1)
                    pool.wait_ge(s["dd"], b + 1)
                    TT(a0[:, :, :], p0[:, :, :], dd[:, :].unsqueeze(2).to_broadcast([P, NH, TOP]), ALU.mult)\
                        .then_inc(s["fa"], 1)
                    pool.wait_ge(s["p2"], b + 1)
                    TT(p0r[:, 2, :], p0r[:, 1, :], dinv[:, :, 0], ALU.mult).then_inc(s["rest"], 1)
                if k in (6, 7) and 0 <= b < B:
                    t = k - 6
                    pool.wait_ge(s["fa"], b + 1)
                    pool.wait_ge(s["es"], b + 1)
                    if b >= 1:
                        pool.wait_ge(s["wt"], b)
                    hs = slice(FH * t, FH * (t + 1))
                    TT(prod[:, t, :, :, :], r_sb[:, hs, 0:NK].unsqueeze(2).to_broadcast([P, FH, TOP, NK]),
                       a0[:, hs, :].unsqueeze(3).to_broadcast([P, FH, TOP, NK]), ALU.mult).then_inc(s["pr"], 1)
                    if t == 1:
                        pool.wait_ge(s["pr"], 4 * b + 2)
                        pool.wait_ge(s["rest"], b + 1)
                        lastx = prod[:, :, :, TOP - 1, NK - 1]
                        TT(lastx, lastx, p0r[:, 2, :].rearrange("p (t h) -> p t h", t=BT), ALU.add).then_inc(s["pr"], 1)
                        pool.wait_ge(s["pr"], 4 * b + 3)
                        TT(prod[:, :, 0:FH // 2, :, :].rearrange("p t h i j -> p t (h i j)"),
                           prod[:, :, 0:FH // 2, :, :].rearrange("p t h i j -> p t (h i j)"),
                           prod[:, :, FH // 2:FH, :, :].rearrange("p t h i j -> p t (h i j)"), ALU.add).then_inc(s["pr"], 1)


NAMES = ["L0_attn_x", "L0_attn_Wq", "L0_attn_bq", "L0_attn_Wl", "L0_attn_bl", "L0_attn_Wk", "L0_attn_bk",
         "L0_attn_Wv", "L0_attn_bv", "L0_attn_Wo", "L0_attn_bo", "L0_ffn_Wq", "L0_ffn_bq", "L0_ffn_bn_gamma",
         "L0_ffn_bn_beta", "L0_ffn_sub_key0", "L0_ffn_sub_key1", "L0_ffn_expert_down", "L0_ffn_expert_up"]


def kernel(**inputs):
    import concourse.bacc as bacc
    from concourse.bass_utils import run_bass_kernel_spmd

    nc = bacc.Bacc("TRN2", target_bir_lowering=False, num_devices=1)
    arrays, args = {}, []
    for name in NAMES:
        a = np.ascontiguousarray(inputs[name])
        arrays[name] = a
        args.append(nc.dram_tensor(name, a.shape, mybir.dt.from_np(a.dtype), kind="ExternalInput").ap())
    arrays["const"] = constants()
    args.append(nc.dram_tensor("const", (P, C_END), F32, kind="ExternalInput").ap())
    shape = inputs["L0_attn_x"].shape
    args.append(nc.dram_tensor("qk_parts", (2, shape[0] // 2, 16, 6, 8, 512), BF16, kind="Internal").ap())
    args.append(nc.dram_tensor("out", shape, F32, kind="ExternalOutput").ap())
    program(nc, *args)
    return run_bass_kernel_spmd(nc, [arrays], core_ids=[0]).results[0]["out"]
```

```python
from contextlib import ExitStack

import numpy as np

import concourse.bass as bass
from concourse import mybir

F32 = mybir.dt.float32
BF16 = mybir.dt.bfloat16
ALU = mybir.AluOpType
ACT = mybir.ActivationFunctionType
AX = mybir.AxisListType.X

P = 128
NEG = -1.0e20

C_ID, C_SEL, C_AVG, C_GRP = 0, 128, 164, 292
C_END = C_GRP + 248


def constants():
    c = np.zeros((P, C_END), np.float32)
    p = np.arange(P)
    c[p, C_ID + p] = 1.0
    for col in range(4):
        for r in range(9):
            c[32 * col + r, C_SEL + 18 * (col % 2) + 9 * (col // 2) + r] = 1.0
    c[:, C_AVG:C_AVG + P] = (p[:, None] % 32 == p[None, :] % 32) / 8.0
    c[p, C_GRP + 120 + p // 16] = 1.0
    return c


def program(nc, x, Wq, bq, Wl, bl, Wk, bk, Wv, bv, Wo, bo,
            fWq, fbq, gamma, beta, key0, key1, down, up, const, scratch, out):
    B, S, D = x.shape
    T = B * S
    NT = T // P
    CH = 512
    NC = T // CH
    TC = CH // P
    BT = S // P
    L = Wl.shape[1]
    H, DH = 16, 8
    NPAIR = H // 2
    SCALE = float(DH) ** -0.5
    VC = DH + 1
    FH, FQ = 8, 32
    G = 2 * FH
    NK = 32
    TOP = 4
    KP = NK + TOP
    E = down.shape[0]
    TERMS = 6
    ROWS = TERMS * DH
    PARTS = 3
    RUNS = (((0, 0, 3), (3, 0, 1), (4, 0, 2)),
            ((0, 0, 2), (2, 0, 3), (5, 0, 1)))
    RING = 4
    LAG = 11
    LN_EPS, BN_EPS, NORM_EPS = 1e-5, 1e-5, 1e-12

    xt = x.rearrange("b (n p) d -> p (b n) d", p=P)
    ot = out.rearrange("b (n p) d -> p (b n) d", p=P)

    ctx = ExitStack()
    with ctx:
        def sb(name, shape, dt=F32):
            return ctx.enter_context(nc.sbuf_tensor(name, shape, dt))

        def sem(name):
            return ctx.enter_context(nc.semaphore(name))

        cst = sb("cst", [P, C_END])
        ident = cst[:, C_ID:C_ID + P]
        sel = cst[:, C_SEL:C_SEL + 36]
        avg = cst[:, C_AVG:C_AVG + P]
        grp = cst[:, C_GRP + 120:C_GRP + 128]
        ident_b = sb("ident_b", [P, P], BF16)
        wq_sb = sb("wq_sb", [P, D]); wl_sb = sb("wl_sb", [P, L]); wkv_in = sb("wkv_in", [L, 2, D])
        wlT = sb("wlT", [L, P]); wkv = sb("wkv", [P, 2, D])
        wo_sb = sb("wo_sb", [P, D])
        fwq_sb = sb("fwq_sb", [P, 2 * P]); down_sb = sb("down_sb", [P, D]); up_sb = sb("up_sb", [P, D])
        downT = sb("downT", [P, E])
        bo_sb = sb("bo_sb", [P, D])
        vecs = sb("vecs", [P, 10])
        keys = sb("keys", [NK, 2, 16])
        keys_sq = sb("keys_sq", [NK, 2, 16])
        keys_n = sb("keys_n", [NK, 2, 3])
        keys_rep = sb("keys_rep", [NK, 4, 2, 16])
        kblk = sb("kblk", [P, 8, NK])
        x_sb = sb("x_sb", [P, NT, D])
        xnT = sb("xnT", [P, T])
        gT = xnT
        st6 = sb("st6", [P, NT, 6]); mv = sb("mv", [P, NT, 2])
        ve = sb("ve", [P, NT]); sd = sb("sd", [P, NT]); rs = sb('rs', [P, NT])
        nm = ve
        vhat = sb("vhat", [P, NT * H * VC + 32])
        parts = sb("parts", [P, 2, 2, 3, CH], BF16)
        fst = sb("fst", [P, 2, NC, 6]); fmv = sb("fmv", [P, 2, 2])
        bnv = sb("bnv", [P, 16])
        fqT = sb("fqT", [P, 2, T])
        rn_t = sb("rn_t", [P, CH]); rn = sb("rn", [P, NT, G])
        QS = sb("QS", [P, RING, 2, NPAIR, S], BF16)
        KS = sb("KS", [P, RING, NPAIR, S], BF16)
        negm = sb("negm", [P, 2, 2, BT, NPAIR])
        mpart = sb("mpart", [P, BT, 2, 2, NPAIR], BF16)
        mT = sb("mT", [2 * H, S], BF16)
        Eb = sb("Eb", [P, 4, 2 * BT * S])
        xn_sb = Eb[:, 0, :].rearrange("p (a t d) -> p a t d", a=2, t=TC)
        sq = Eb[:, 1, :].rearrange("p (r n) -> p r n", r=2)
        q32 = Eb[:, 2, :].rearrange("p (r n) -> p r n", r=2)
        r32 = Eb[:, 3, :].rearrange("p (r n) -> p r n", r=2)
        Osb = sb("Osb", [P, 4, S])
        rden = sb("rden", [P, BT * H]); on = sb("on", [P, BT, D]); onT = sb("onT", [P, S])
        ysb = sb("ysb", [P, 2, BT, D])
        NH = BT * FH
        s_sb = sb("s_sb", [P, NH, 2, KP]); r_sb = sb("r_sb", [P, NH, KP])
        top8 = sb("top8", [P, NH, 2, 8]); top4 = sb("top4", [P, NH, 8])
        ZW = NK + 3 * TOP
        z_sb = sb("z_sb", [P, NH, ZW])
        den = sb("den", [P, NH, 2]); dinv = sb("dinv", [P, NH, 2])
        cmp = sb("cmp", [P, NH, TOP, TOP]); cm2 = sb("cm2", [P, NH, TOP, 2])
        ties = sb("ties", [P, NH, 6]); rank = sb("rank", [P, 4, NH, TOP])
        p0 = sb("p0", [P, NH, TOP]); p0s = sb("p0s", [P, NH, 2]); p0r = sb("p0r", [P, 3, NH])
        dd = sb("dd", [P, NH]); a0 = sb("a0", [P, NH, TOP])
        prod = sb("prod", [P, BT, FH, TOP, NK])
        wgT = sb("wgT", [P, S])

        bank = [ctx.enter_context(nc.psum_tensor(f"bank{i}", [P, 512], F32)) for i in range(4)]
        SJ = [ctx.enter_context(nc.psum_tensor(f"SJ{i}", [P, 1024], F32)) for i in range(2)]
        SI = [bank[0][:, :], bank[1][:, :]]
        psO, psM = bank[2][:, :], bank[3][:, :]
        psX = [psO, SJ[1][:, 512:1024]]
        psQ, psK, psV = SJ[0][:, 0:512], SJ[0][:, 512:1024], SJ[1][:, 0:512]
        psW = psQ
        psF = [SI, [psM, psV]]
        psN = psO
        psG = [SJ[1][:, 0:512], SJ[1][:, 512:1024]]

        names = ("w0 w w2 stats aggr var std rstd nm xn xn2 xT xnT q q_ev k k_ev v v_ev f f_ev f_st "
                 "hi_q hi_k r_q r_k mid_q mid_k lo_q lo_k spill0 spill1 kn1 kn2 kn3 kn4 kn5 krep kmm kblk dT downT "
                 "bn ba bb bc bd g g_ev ff sq n2 n2s n2c rn n2r rnT bb1 wl wl_ev wkv wkv_ev vone kone qzero pad identb "
                 "si mx mh ms mt mt_ev mrow sj ex pv o_ev ct rd on onp onT y fin st0 st1 "
                 "fs fs_ev t8 t4 mr z ze es fd fe cmp c2 tie rk sel p0 ps p1 p2 dd fa rest pr wt wg xb").split()
        s = {n: sem("s_" + n) for n in names}
        s_x = [sem(f"s_x{c}") for c in range(NC)]
        s_load = [sem(f"s_load{i}") for i in range(RING)]

        block = ctx.enter_context(nc.Block())
        NSLOT = NPAIR * B + LAG + 6

        def col(v):
            return v.rearrange("(p a) -> p a", a=1)

        def four(v):
            return col(v).unsqueeze(0).to_broadcast([4, FQ, 1])

        W0LOADS = [(cst[:, :], const), (fwq_sb[:, :], fWq)]
        WLOADS = [(wl_sb[:, :], Wl), (wq_sb[:, :], Wq), (wkv_in[:, 0, :], Wk),
                  (vecs[0:L, 6:7], col(bl)), (vecs[:, 0:1], col(bq)), (vecs[:, 1:2], col(bk)),
                  (wkv_in[:, 1, :], Wv), (vecs[:, 7:8], col(bv))]
        W2LOADS = [(vecs[:, 4:5], col(fbq[0:P])), (vecs[:, 5:6], col(fbq[P:2 * P])),
                   (vecs[:, 2:3], four(gamma)), (vecs[:, 3:4], four(beta)),
                   (wo_sb[:, :], Wo), (down_sb[:, :], down), (up_sb[:, :], up),
                   (keys[:, 0, :], key0), (keys[:, 1, :], key1),
                   (bo_sb[:, :], bo.rearrange("(a n) -> a n", a=1).to_broadcast([P, D]))]
        NW0, NW, NW2 = (16 * len(w) for w in (W0LOADS, WLOADS, W2LOADS))
        NSPILL = 2 * PARTS
        NLOAD = 2 * sum(len(runs) for runs in RUNS)

        @block.sync
        def _(sp):
            for c in range(NC):
                sp.dma_start(x_sb[:, TC * c:TC * (c + 1), :], xt[:, TC * c:TC * (c + 1), :]).then_inc(s_x[c], 16)
                if c == 1:
                    for dst, src in W0LOADS:
                        sp.dma_start(dst, src).then_inc(s["w0"], 16)
                if c == 3:
                    for dst, src in WLOADS:
                        sp.dma_start(dst, src).then_inc(s["w"], 16)
            for dst, src in W2LOADS:
                sp.dma_start(dst, src).then_inc(s["w2"], 16)

            def spill(c):
                for t in range(2):
                    sp.wait_ge(s["lo_q" if t == 0 else "lo_k"], c + 1)
                    for part in range(PARTS):
                        sp.dma_start(scratch[t, c, :, part],
                                     parts[:, c % 2, t, part, :]).then_inc(s[f"spill{c % 2}"], 16)

            def store(b):
                sp.wait_ge(s["fin"], b + 1)
                sp.dma_start(ot[:, BT * b:BT * (b + 1), :], ysb[:, b % 2, :, :]).then_inc(s[f"st{b % 2}"], 16)

            def load(b):
                c, o = b // 2, (b % 2) * S
                sp.wait_ge(s[f"spill{c % 2}"], 16 * NSPILL * (c // 2 + 1))
                if b >= RING:
                    sp.wait_ge(s["sj"], NPAIR * (b - RING + 1))
                for e in range(2):
                    for t, dst in ((0, QS[:, b % RING, e]), (1, KS[:, b % RING])):
                        for term, part, length in RUNS[t]:
                            r0 = 64 * e + DH * term
                            src = scratch[t, c, NPAIR * e:NPAIR * (e + 1), part:part + length].rearrange("r a d n -> (a d) r n")
                            sp.dma_start(dst[r0:r0 + DH * length], src[:, :, o:o + S]).then_inc(s_load[b % RING], 16)

            def max_rows(b):
                sp.wait_ge(s["mt_ev"], b + 1)
                for e in range(2):
                    for part in range(2):
                        src = (e * 2 + part) * NPAIR
                        r0 = 64 * e + ROWS + part
                        sp.dma_start(QS[r0:r0 + 1, b % RING, e, :, :], mT[src:src + NPAIR, :]).then_inc(s["mrow"], 16)

            sp.wait_ge(s["kone"], 1)
            sp.wait_ge(s["qzero"], 1)
            spill(0)
            load(0)
            load(1)
            for c in range(1, NC):
                spill(c)
            load(2)
            for it in range(1, B + 4):
                if it <= B:
                    max_rows(it - 1)
                if it + 2 < B:
                    load(it + 2)
                if it >= 4:
                    store(it - 4)
            for e in range(2):
                sp.wait_ge(s[f"st{e}"], 16 * B // 2)

        @block.scalar
        def _(act):
            A = nc.scalar.activation

            def v_rows(c):
                act.wait_ge(s["v"], c + 1)
                act.wait_ge(s["vone"], 1)
                A(vhat[:, TC * c * H * VC:TC * (c + 1) * H * VC].rearrange("p (n v) -> p n v", v=VC)[:, :, 0:DH],
                  psV.rearrange("p (n v) -> p n v", v=DH), ACT.Copy).then_inc(s["v_ev"], 1)

            def split(c):
                if c >= 2:
                    act.wait_ge(s[f"spill{c % 2}"], 16 * NSPILL * (c // 2))
                for t, nm in enumerate(("q", "k")):
                    act.wait_ge(s[nm + "_ev"], c + 1)
                    A(parts[:, c % 2, t, 0, :], q32[:, t, :], ACT.Copy).then_inc(s["hi_" + nm], 1)
                for t, nm in enumerate(("q", "k")):
                    act.wait_ge(s["r_" + nm], c + 1)
                    A(parts[:, c % 2, t, 1, :], r32[:, t, :], ACT.Copy).then_inc(s["mid_" + nm], 1)

            for c in range(-1, NC + 2):
                if 0 <= c < NC:
                    act.wait_ge(s["nm"], c + 1)
                    if c >= 2:
                        act.wait_ge(s["xT"], c - 1)
                    for t in range(TC // 2):
                        n = TC * c + t
                        last = A(xn_sb[:, c % 2, t, :], x_sb[:, n, :], ACT.Identity, bias=nm[:, n:n + 1], scale=rs[:, n:n + 1])
                    last.then_inc(s["xn"], 1)
                if c >= 2:
                    for r in range(2):
                        act.wait_ge(s["f"], 2 * (c - 2) + r + 1)
                        A(fqT[:, r, (c - 2) * CH:(c - 1) * CH], psF[c % 2][r], ACT.Copy).then_inc(s["f_ev"], 1)
                if 1 <= c <= NC:
                    act.wait_ge(s["xT"], c)
                    A(xnT[:, (c - 1) * CH:c * CH], psX[(c - 1) % 2], ACT.Copy).then_inc(s["xnT"], 1)
                if c + 1 < NC:
                    act.wait_ge(s["var"], c + 2)
                    A(sd[:, TC * (c + 1):TC * (c + 2)], ve[:, TC * (c + 1):TC * (c + 2)], ACT.Sqrt).then_inc(s["std"], 1)
                if c == 3:
                    act.wait_ge(s["wl"], 1)
                    A(wlT[:, :], psW[0:L, 0:P], ACT.Copy).then_inc(s["wl_ev"], 1)
                if c == 4:
                    act.wait_ge(s["wkv"], 1)
                    act.wait_ge(s["w"], NW)
                    A(wkv[:, :, :], psW[:, 0:2 * D].rearrange("p (a d) -> p a d", a=2), ACT.Copy)
                    A(vecs[:, 8:9], psW[:, 2 * D:2 * D + 1], ACT.Identity, bias=vecs[:, 1:2])
                    A(vecs[:, 9:10], psW[:, 2 * D + 1:2 * D + 2], ACT.Identity, bias=vecs[:, 7:8]).then_inc(s["wkv_ev"], 1)
                if c == NC - 1:
                    act.wait_ge(s["kn2"], 1)
                    A(keys_n[:, :, 1], keys_n[:, :, 0], ACT.Sqrt).then_inc(s["kn3"], 1)
                if c == 6:
                    split(0)

            for slot in range(NSLOT):
                k = slot % 8
                if slot == 0:
                    v_rows(0)
                    v_rows(1)
                    split(1)
                    act.wait_ge(s["bc"], 1)
                    A(bnv[:, 6:7], bnv[:, 5:6], ACT.Sqrt).then_inc(s["bd"], 1)
                if slot < NC:
                    act.wait_ge(s["ff"], slot + 1)
                    if slot >= 1:
                        act.wait_ge(s["n2"], slot)
                    A(sq[:, :, :], fqT[:, :, slot * CH:(slot + 1) * CH], ACT.Square).then_inc(s["sq"], 1)
                if 1 <= slot < NC - 1:
                    v_rows(slot + 1)
                    split(slot + 1)
                if slot == NC:
                    act.wait_ge(s["n2"], NC)
                    A(rn_t[:, :], psN, ACT.Sqrt).then_inc(s["n2s"], 1)
                b = slot // 8 - 1
                if k == 1 and 0 <= b < B:
                    act.wait_ge(s["mt"], b + 1)
                    if b >= 1:
                        act.wait_ge(s["mrow"], 64 * b)
                    A(mT[:, :], psM[0:2 * H, 0:S], ACT.Copy).then_inc(s["mt_ev"], 1)
                if k in (2, 3) and 0 <= b < B:
                    t = k - 2
                    act.wait_ge(s["fs"], 2 * b + t + 1)
                    act.wait_ge(s["pad"], 1)
                    if b >= 1:
                        act.wait_ge(s["mr"], 2 * b)
                        act.wait_ge(s["sel"], b)
                    A(s_sb[:, FH * t:FH * (t + 1), :, 0:NK].rearrange("p h a k -> p (h a) k"),
                      psM.rearrange("p (g k) -> p g k", k=NK), ACT.Copy).then_inc(s["fs_ev"], 1)
                m = slot - LAG - 4
                if m >= 0 and m % 2 == 0 and m // 2 < 4 * B:
                    g = m // 2
                    act.wait_ge(s["pv"], g + 1)
                    if g >= 4:
                        act.wait_ge(s["ct"], g // 4)
                    A(Osb[:, g % 4, :], psO[:, (g % 2) * S:(g % 2 + 1) * S], ACT.Copy).then_inc(s["o_ev"], 1)
                ba = (slot - LAG - 12) // 8
                if k == 7 and 0 <= ba < B:
                    act.wait_ge(s["onp"], ba + 1)
                    if ba >= 1:
                        act.wait_ge(s["y"], ba)
                    A(onT[:, :], psM[:, 0:S], ACT.Identity, bias=vecs[:, 9:10]).then_inc(s["onT"], 1)
                n = slot - LAG
                if 0 <= n < NPAIR * B:
                    act.wait_ge(s["sj"], n + 1)
                    if n >= 4:
                        act.wait_ge(s["pv"], (n - 4) // 2 + 1)
                    elif n == 0:
                        act.wait_ge(s["lo_q"], NC)
                        act.wait_ge(s["lo_k"], NC)
                    A(Eb[:, n % 4, :], SJ[n % 2][:, :], ACT.Exp).then_inc(s["ex"], 1)
                if slot in (NC, NC + 1):
                    for c in range(4 * (slot - NC), 4 * (slot - NC + 1)):
                        act.wait_ge(s["g"], c + 1)
                        A(gT[:, c * CH:(c + 1) * CH], psG[c % 2], ACT.Gelu).then_inc(s["g_ev"], 1)
                if k == 5 and 0 <= b < B:
                    act.wait_ge(s["z"], b + 1)
                    A(z_sb[:, :, :], z_sb[:, :, :], ACT.Exp).then_inc(s["ze"], 1)

        @block.tensor
        def _(pe):
            mm = nc.tensor.matmul

            def project_qk(c):
                xc = xnT[:, c * CH:(c + 1) * CH]
                if c >= 1:
                    pe.wait_ge(s["q_ev"], c)
                mm(psQ, wq_sb[:, :], xc, start=True, stop=True).then_inc(s["q"], 1)
                if c >= 1:
                    pe.wait_ge(s["k_ev"], c)
                mm(psK, wkv[:, 0, :], xc, start=True, stop=True).then_inc(s["k"], 1)

            def project_v(c):
                xc = xnT[:, c * CH:(c + 1) * CH]
                if c == 0:
                    pe.wait_ge(s["f_ev"], 2 * NC)
                else:
                    pe.wait_ge(s["v_ev"], c)
                for t in range(TC):
                    last = mm(psV[:, t * P:(t + 1) * P], xc[:, t * P:(t + 1) * P], wkv[:, 1, :], start=True, stop=True)
                last.then_inc(s["v"], 1)

            pe.wait_ge(s["w0"], NW0)
            for c in range(NC + 1):
                if c < NC:
                    pe.wait_ge(s["xn"], c + 1)
                    pe.wait_ge(s["xn2"], c + 1)
                    if c >= 2:
                        pe.wait_ge(s["xnT"], c - 1)
                    for t in range(TC):
                        last = mm(psX[c % 2][:, t * P:(t + 1) * P], xn_sb[:, c % 2, t, :], ident, start=True, stop=True)
                    last.then_inc(s["xT"], 1)
                if c >= 1:
                    pe.wait_ge(s["xnT"], c)
                    for r in range(2):
                        if c >= 3:
                            pe.wait_ge(s["f_ev"], 2 * (c - 3) + r + 1)
                        mm(psF[(c - 1) % 2][r], fwq_sb[:, r * P:(r + 1) * P], xnT[:, (c - 1) * CH:c * CH],
                           start=True, stop=True).then_inc(s["f"], 1)
                if c == 2:
                    pe.wait_ge(s["w"], NW)
                    mm(psW[0:L, 0:P], wl_sb[:, :], ident, start=True, stop=True).then_inc(s["wl"], 1)
                if c == 3:
                    pe.wait_ge(s["wl_ev"], 1)
                    mm(psW[:, 0:2 * D], wlT[:, :], wkv_in[:, :, :].rearrange("p a d -> p (a d)"), start=True, stop=True)
                    for a in range(2):
                        last = mm(psW[:, 2 * D + a:2 * D + a + 1], wkv_in[:, a, :], vecs[0:L, 6:7], start=True, stop=True)
                    last.then_inc(s["wkv"], 1)
                if c == 5:
                    pe.wait_ge(s["wkv_ev"], 1)
                    project_qk(0)
            project_qk(1)
            project_v(0)
            project_v(1)
            pe.wait_ge(s["xnT"], NC)
            pe.wait_ge(s["w2"], NW2)
            mm(psX[0][:, 0:E], down_sb[:, :], ident, start=True, stop=True).then_inc(s["dT"], 1)
            pe.wait_ge(s["krep"], 1)
            mm(psX[1][:, 0:NK], keys_rep[:, :, :, :].rearrange("k h a d -> k (h a d)"), cst[0:NK, 0:NK],
               start=True, stop=True).then_inc(s["kmm"], 1)
            pe.wait_ge(s["identb"], 1)

            def bn_mean():
                pe.wait_ge(s["ba"], 1)
                pe.wait_ge(s["downT"], 1)
                for r in range(2):
                    last = mm(psX[0][:, 0:1], avg, bnv[:, r:r + 1], start=(r == 0), stop=(r == 1))
                last.then_inc(s["ba"], 1)

            def bn_variance():
                pe.wait_ge(s["bb"], 1)
                for r in range(2):
                    last = mm(psX[0][:, 2:3], avg, bnv[:, 2 + r:3 + r], start=(r == 0), stop=(r == 1))
                last.then_inc(s["bb"], 1)
                pe.wait_ge(s["bc"], 1)

            def si(n):
                b, pr = n // NPAIR, n % NPAIR
                if pr == 0:
                    pe.wait_ge(s_load[b % RING], 16 * NLOAD * (b // RING + 1))
                for e in range(2):
                    if n >= 1:
                        pe.wait_ge(s["mx"], 2 * (n - 1) + e + 1)
                    else:
                        pe.wait_ge(s["f_ev"], 2 * NC)
                    r = slice(64 * e, 64 * e + ROWS)
                    for t in range(BT):
                        last = mm(SI[e][:, t * S:(t + 1) * S], QS[r, b % RING, e, pr, t * P:(t + 1) * P],
                                  KS[r, b % RING, pr, :], start=True, stop=True)
                    last.then_inc(s["si"], 1)

            def norms(c):
                pe.wait_ge(s["sq"], c + 1)
                for r in range(2):
                    at = C_GRP + 120 - (c * G + 8 * r)
                    last = mm(psN, cst[:, at:at + P], sq[:, r, :], start=(c + r == 0), stop=(c == NC - 1 and r == 1),
                              skip_group_check=True)
                last.then_inc(s["n2"], 1)

            for slot in range(NSLOT):
                k = slot % 8
                if 1 <= slot < NC - 1:
                    project_qk(slot + 1)
                    project_v(slot + 1)
                if slot == 0:
                    bn_mean()
                if slot < NPAIR * B:
                    si(slot)
                if slot == 0:
                    bn_variance()
                if 1 <= slot <= NC:
                    norms(slot - 1)
                if slot == NC + 1:
                    pe.wait_ge(s["n2r"], 1)
                    for t in range(TC):
                        last = mm(psN[:, t * P:(t + 1) * P], rn_t[:, t * P:(t + 1) * P], ident, start=True, stop=True)
                    last.then_inc(s["rnT"], 1)
                n = slot - LAG
                if 0 <= n < NPAIR * B:
                    b, pr = n // NPAIR, n % NPAIR
                    if pr == 0:
                        pe.wait_ge(s["mrow"], 64 * (b + 1))
                    if n >= 2:
                        pe.wait_ge(s["ex"], n - 1)
                    else:
                        pe.wait_ge(s["k_ev"], NC)
                        pe.wait_ge(s["g_ev"], NC)
                    for e in range(2):
                        for t in range(BT):
                            last = mm(SJ[n % 2][:, (e * BT + t) * S:(e * BT + t + 1) * S],
                                      KS[:, b % RING, pr, t * P:(t + 1) * P],
                                      QS[:, b % RING, e, pr, :], start=True, stop=True)
                    last.then_inc(s["sj"], 1)
                m = slot - LAG - 3
                if m >= 0 and m % 2 == 0 and m // 2 < 4 * B:
                    g = m // 2
                    b = g // 4
                    pe.wait_ge(s["ex"], 2 * g + 2)
                    if g >= 1:
                        pe.wait_ge(s["o_ev"], g)
                    else:
                        pe.wait_ge(s["rn"], 1)
                        pe.wait_ge(s["v_ev"], NC)
                    for t in range(BT):
                        for c in range(4):
                            h = 2 * (g % 4) + c // 2 + NPAIR * (c % 2)
                            v0 = ((BT * b + t) * H + h) * VC
                            e0 = ((c % 2) * BT + t) * S
                            last = mm(psO[32 * c:32 * c + 32, (g % 2) * S:(g % 2 + 1) * S], vhat[:, v0:v0 + 32],
                                      Eb[:, (2 * g + c // 2) % 4, e0:e0 + S], start=(t == 0), stop=(t == BT - 1),
                                      tile_position=(0, 32 * c), skip_group_check=True)
                    last.then_inc(s["pv"], 1)
                b = slot // 8 - 1
                if k == 0 and 0 <= b < B:
                    pe.wait_ge(s["ms"], b + 1)
                    if b >= 2:
                        pe.wait_ge(s["fin"], b - 1)
                    for t in range(BT):
                        last = mm(psM[0:2 * H, t * P:(t + 1) * P], mpart[:, t, :, :, :].rearrange("p e a r -> p (e a r)"),
                                  ident_b[:, :], start=True, stop=True)
                    last.then_inc(s["mt"], 1)
                if k in (1, 2) and 0 <= b < B:
                    t = k - 1
                    if t == 0:
                        pe.wait_ge(s["mt_ev"], b + 1)
                    else:
                        pe.wait_ge(s["fs_ev"], 2 * b + 1)
                    tok = (BT * b + t) * P
                    for r in range(2):
                        last = mm(psM[:, 256 * r:256 * (r + 1)], fqT[:, r, tok:tok + P],
                                  kblk[:, :, :].rearrange("p g k -> p (g k)"), start=True, stop=True)
                    last.then_inc(s["fs"], 1)
                if slot in (NC, NC + 1):
                    for c in range(4 * (slot - NC), 4 * (slot - NC + 1)):
                        if c >= 2:
                            pe.wait_ge(s["g_ev"], c - 1)
                        else:
                            pe.wait_ge(s["v_ev"], NC)
                            pe.wait_ge(s["kblk"], 1)
                        mm(psG[c % 2], downT[:, :], xnT[:, c * CH:(c + 1) * CH], start=True, stop=True).then_inc(s["g"], 1)
                b = (slot - LAG - 8) // 8
                if k == 3 and 0 <= b < B:
                    pe.wait_ge(s["pr"], 4 * (b + 1))
                    if b + 1 < B:
                        pe.wait_ge(s["fs_ev"], 2 * (b + 2))
                    else:
                        pe.wait_ge(s["fin"], b)
                    for t in range(BT):
                        for h in range(FH // 2):
                            last = mm(psM[:, t * P:(t + 1) * P], prod[:, t, h, :, :].rearrange("p i j -> p (i j)"), ident,
                                      start=(h == 0), stop=(h == FH // 2 - 1))
                    last.then_inc(s["wt"], 1)
                b = (slot - LAG - 10) // 8
                if k == 5 and 0 <= b < B:
                    pe.wait_ge(s["wg"], b + 1)
                    pe.wait_ge(s["o_ev"], 4 * (b + 1))
                    for t in range(BT):
                        for g in range(4):
                            ct = psM[:, t * H * VC:(t + 1) * H * VC].rearrange("p (e n) -> p e n", e=2)
                            last = mm(ct[:, :, 2 * g * VC:2 * (g + 1) * VC], Osb[:, g, t * P:(t + 1) * P],
                                      sel, start=True, stop=True)
                    last.then_inc(s["ct"], 1)
                b = (slot - LAG - 11) // 8
                if k == 6 and 0 <= b < B:
                    pe.wait_ge(s["on"], b + 1)
                    for t in range(BT):
                        last = mm(psM[:, t * P:(t + 1) * P], on[:, t, :], ident, start=True, stop=True)
                    last.then_inc(s["onp"], 1)
                b = (slot - LAG - 12) // 8
                if k == 7 and 0 <= b < B:
                    pe.wait_ge(s["onT"], b + 1)
                    for t in range(BT):
                        mm(psM[:, t * D:(t + 1) * D], onT[:, t * P:(t + 1) * P], wo_sb[:, :], start=True, stop=False)
                        last = mm(psM[:, t * D:(t + 1) * D], wgT[:, t * P:(t + 1) * P], up_sb[:, :], start=False, stop=True)
                    last.then_inc(s["y"], 1)

        @block.vector
        def _(dve):
            V = nc.vector
            step = [0]

            def chain(i):
                step[0] += 1
                i.then_inc(s["bb1"], 1)
                dve.wait_ge(s["bb1"], step[0])

            def q_ev(c):
                dve.wait_ge(s["q"], c + 1)
                if c == 0:
                    dve.wait_ge(s["w"], NW)
                if c >= 1:
                    dve.wait_ge(s["r_q"], c)
                    dve.wait_ge(s["hi_q"], c)
                V.tensor_scalar(q32[:, 0, :], psQ, vecs[:, 0:1], SCALE, ALU.add, ALU.mult).then_inc(s["q_ev"], 1)

            def k_ev(c):
                dve.wait_ge(s["k"], c + 1)
                if c >= 1:
                    dve.wait_ge(s["r_k"], c)
                    dve.wait_ge(s["hi_k"], c)
                V.tensor_scalar(q32[:, 1, :], psK, vecs[:, 8:9], None, ALU.add).then_inc(s["k_ev"], 1)

            def lo_k(c):
                dve.wait_ge(s["mid_k"], c + 1)
                V.tensor_tensor(parts[:, c % 2, 1, 2, :], r32[:, 1, :], parts[:, c % 2, 1, 1, :], ALU.subtract)\
                    .then_inc(s["lo_k"], 1)

            def unit_keys():
                dve.wait_ge(s["kn3"], 1)
                V.tensor_scalar(keys_n[:, :, 2], keys_n[:, :, 1], NORM_EPS, None, ALU.max).then_inc(s["kn4"], 1)
                dve.wait_ge(s["kn4"], 1)
                V.reciprocal(keys_n[:, :, 0], keys_n[:, :, 2]).then_inc(s["kn5"], 1)
                dve.wait_ge(s["kn5"], 1)
                for h in range(4):
                    last = V.tensor_tensor(keys_rep[:, h, :, :], keys[:, :, :],
                                           keys_n[:, :, 0:1].to_broadcast([NK, 2, 16]), ALU.mult)
                last.then_inc(s["krep"], 1)

            for c in range(-1, NC + 3):
                if 0 <= c < NC:
                    dve.wait_ge(s["std"], c + 1)
                    V.reciprocal(rs[:, TC * c:TC * (c + 1)], sd[:, TC * c:TC * (c + 1)]).then_inc(s["rstd"], 1)
                    dve.wait_ge(s["rstd"], c + 1)
                    V.scalar_tensor_tensor(nm[:, TC * c:TC * (c + 1)], mv[:, TC * c:TC * (c + 1), 0], -1.0,
                                           rs[:, TC * c:TC * (c + 1)], ALU.mult, ALU.mult).then_inc(s["nm"], 1)
                    if c >= 2:
                        dve.wait_ge(s["xT"], c - 1)
                    for t in range(TC // 2, TC):
                        n = TC * c + t
                        last = V.tensor_scalar(xn_sb[:, c % 2, t, :], x_sb[:, n, :], mv[:, n, 0:1], rs[:, n:n + 1],
                                               ALU.subtract, ALU.mult)
                    last.then_inc(s["xn2"], 1)
                if c + 1 < NC:
                    dve.wait_ge(s_x[c + 1], 16)
                    tiles = range(TC * (c + 1), TC * (c + 2))
                    for n in tiles:
                        last = V.bn_stats(st6[:, n, :], x_sb[:, n, :])
                    last.then_inc(s["stats"], 1)
                    dve.wait_ge(s["stats"], c + 2)
                    for n in tiles:
                        last = V.bn_aggr(mv[:, n, :], st6[:, n, :])
                    last.then_inc(s["aggr"], 1)
                    dve.wait_ge(s["aggr"], c + 2)
                    V.tensor_scalar(ve[:, TC * (c + 1):TC * (c + 2)], mv[:, TC * (c + 1):TC * (c + 2), 1],
                                    LN_EPS, None, ALU.add).then_inc(s["var"], 1)
                if c == 6:
                    q_ev(0)
                    k_ev(0)
                if c >= 3:
                    for r in range(2):
                        dve.wait_ge(s["f_ev"], 2 * (c - 3) + r + 1)
                        V.bn_stats(fst[:, r, c - 3, :], fqT[:, r, (c - 3) * CH:(c - 2) * CH]).then_inc(s["f_st"], 1)
                if c == 5:
                    dve.wait_ge(s["w0"], NW0)
                    V.tensor_copy(ident_b[:, :], ident).then_inc(s["identb"], 1)
                    dve.wait_ge(s["w2"], NW2)
                    V.tensor_tensor(keys_sq[:, :, :], keys[:, :, :], keys[:, :, :], ALU.mult).then_inc(s["kn1"], 1)
                    dve.wait_ge(s["kn1"], 1)
                    V.tensor_reduce(keys_n[:, :, 0], keys_sq[:, :, :], axis=AX, op=ALU.add).then_inc(s["kn2"], 1)
                if c == NC - 1:
                    lo_k(0)
                if c == NC:
                    unit_keys()

            q_ev(1)
            dve.wait_ge(s["f_st"], 2 * NC)
            for r in range(2):
                last = V.bn_aggr(fmv[:, r, :], fst[:, r, :, :])
            chain(last)
            V.tensor_tensor(bnv[:, 0:2], fmv[:, :, 0], vecs[:, 4:6], ALU.add).then_inc(s["ba"], 1)
            dve.wait_ge(s["dT"], 1)
            V.tensor_copy(downT[:, :], psX[0][:, 0:E]).then_inc(s["downT"], 1)
            dve.wait_ge(s["kmm"], 1)
            V.tensor_tensor(kblk[:, :, :], psX[1][:, 0:NK].unsqueeze(1).to_broadcast([P, 8, NK]),
                            grp.unsqueeze(2).to_broadcast([P, 8, NK]), ALU.mult).then_inc(s["kblk"], 1)
            k_ev(1)

            def bn_solve():
                dve.wait_ge(s["ba"], 2)
                chain(V.tensor_copy(bnv[:, 4:5], psX[0][:, 0:1]))
                chain(V.tensor_scalar(bnv[:, 10:12], bnv[:, 0:2], bnv[:, 4:5], None, ALU.subtract))
                chain(V.tensor_tensor(bnv[:, 12:14], bnv[:, 10:12], bnv[:, 10:12], ALU.mult))
                V.tensor_tensor(bnv[:, 2:4], bnv[:, 12:14], fmv[:, :, 1], ALU.add).then_inc(s["bb"], 1)
                dve.wait_ge(s["bb"], 2)
                V.tensor_scalar(bnv[:, 5:6], psX[0][:, 2:3], BN_EPS, None, ALU.add).then_inc(s["bc"], 1)
                dve.wait_ge(s["bd"], 1)
                chain(V.reciprocal(bnv[:, 14:15], bnv[:, 6:7]))
                V.tensor_scalar(bnv[:, 10:12], vecs[:, 4:6], bnv[:, 4:5], None, ALU.subtract)
                chain(V.tensor_tensor(bnv[:, 7:8], bnv[:, 14:15], vecs[:, 2:3], ALU.mult))
                V.tensor_scalar(bnv[:, 8:10], bnv[:, 10:12], bnv[:, 7:8], vecs[:, 3:4], ALU.mult, ALU.add).then_inc(s["bn"], 1)
                dve.wait_ge(s["bn"], 1)

            for slot in range(NSLOT):
                k = slot % 8
                b = (slot - LAG - 9) // 8
                if k == 4 and 0 <= b < B:
                    dve.wait_ge(s["wt"], b + 1)
                    dve.wait_ge(s["g_ev"], NC)
                    if b >= 1:
                        dve.wait_ge(s["y"], b)
                    V.tensor_tensor(wgT[:, :], psM[:, 0:S], gT[:, b * S:(b + 1) * S], ALU.mult).then_inc(s["wg"], 1)
                b = (slot - LAG - 11) // 8
                if k == 6 and 0 <= b < B:
                    dve.wait_ge(s["ct"], b + 1)
                    ct = psM[:, 0:BT * H * VC].rearrange("p (h v) -> p h v", v=VC)
                    if b >= 1:
                        dve.wait_ge(s["onp"], b)
                    V.reciprocal(rden[:, :], ct[:, :, DH]).then_inc(s["rd"], 1)
                    dve.wait_ge(s["rd"], b + 1)
                    V.tensor_tensor(on[:, :, :].rearrange("p t (h v) -> p (t h) v", v=DH), ct[:, :, 0:DH],
                                    rden[:, :].unsqueeze(2).to_broadcast([P, BT * H, DH]), ALU.mult).then_inc(s["on"], 1)
                b = (slot - LAG - 13) // 8
                if k == 0 and 0 <= b < B:
                    dve.wait_ge(s["y"], b + 1)
                    dve.wait_ge(s["xb"], 1)
                    if b >= 2:
                        dve.wait_ge(s[f"st{b % 2}"], 16 * (b // 2))
                    V.tensor_tensor(ysb[:, b % 2, :, :], psM[:, 0:S].rearrange("p (t d) -> p t d", t=BT),
                                    x_sb[:, BT * b:BT * (b + 1), :], ALU.add).then_inc(s["fin"], 1)
                b = slot // 8 - 1
                if k == 0 and 0 <= b < B:
                    dve.wait_ge(s["mx"], 2 * NPAIR * (b + 1))
                    if b >= 1:
                        dve.wait_ge(s["mt"], b)
                    src = negm[:, b % 2, :, :, :].rearrange("p e t r -> p t e r")
                    V.tensor_copy(mpart[:, :, :, 0, :], src).then_inc(s["mh"], 1)
                    dve.wait_ge(s["mh"], b + 1)
                    V.tensor_tensor(mpart[:, :, :, 1, :], src, mpart[:, :, :, 0, :], ALU.subtract).then_inc(s["ms"], 1)
                if slot == 0:
                    bn_solve()
                if slot < NC:
                    fc = fqT[:, :, slot * CH:(slot + 1) * CH]
                    for r in range(2):
                        last = V.tensor_scalar(fc[:, r, :], fc[:, r, :], bnv[:, 7:8], bnv[:, 8 + r:9 + r], ALU.mult, ALU.add)
                    last.then_inc(s["ff"], 1)
                if 1 <= slot < NC - 1:
                    q_ev(slot + 1)
                if slot < NPAIR * B:
                    bb, pr = slot // NPAIR, slot % NPAIR
                    for e in range(2):
                        dve.wait_ge(s["si"], 2 * slot + e + 1)
                        V.tensor_reduce(negm[:, bb % 2, e, :, pr], SI[e].rearrange("p (t j) -> p t j", j=S),
                                        axis=AX, op=ALU.max, negate=True).then_inc(s["mx"], 1)
                if 1 <= slot < NC - 1:
                    k_ev(slot + 1)
                if 1 <= slot < NC:
                    lo_k(slot)
                if slot == NC:
                    dve.wait_ge(s["n2s"], 1)
                    V.tensor_scalar(rn_t[:, :], rn_t[:, :], NORM_EPS, None, ALU.max).then_inc(s["n2c"], 1)
                    dve.wait_ge(s["n2c"], 1)
                    V.reciprocal(rn_t[:, :], rn_t[:, :]).then_inc(s["n2r"], 1)
                if slot == NC + 2:
                    dve.wait_ge(s["rnT"], 1)
                    V.tensor_copy(rn[:, :, :].rearrange("p (c t) g -> p t c g", t=TC),
                                  psN.rearrange("p (t c g) -> p t c g", t=TC, g=G)).then_inc(s["rn"], 1)
                if k in (2, 3) and 0 <= b < B:
                    t = k - 2
                    dve.wait_ge(s["fs_ev"], 2 * b + t + 1)
                    if b >= 1:
                        dve.wait_ge(s["sel"], b)
                        dve.wait_ge(s["t4"], 2 * b)
                    for h in range(FH * t, FH * (t + 1)):
                        for a in range(2):
                            last = V.max(top8[:, h, a, :], s_sb[:, h, a, 0:NK])
                    last.then_inc(s["t8"], 1)
                if k in (4, 5) and 0 <= b < B:
                    t = k - 4
                    dve.wait_ge(s["t4"], 2 * b + t + 1)
                    if b >= 1:
                        dve.wait_ge(s["pr"], 4 * b)
                    for h in range(FH * t, FH * (t + 1)):
                        last = V.match_replace(r_sb[:, h, :], top4[:, h, :], s_sb[:, h, 1, :], NEG)
                    last.then_inc(s["mr"], 1)
                if k == 6 and 0 <= b < B:
                    dve.wait_ge(s["ze"], b + 1)
                    dve.wait_ge(s["mr"], 2 * b + 2)
                    if b >= 1:
                        dve.wait_ge(s["fa"], b)
                        dve.wait_ge(s["rest"], b)
                    V.tensor_reduce(den[:, :, :], z_sb[:, :, NK + TOP:ZW].rearrange("p h (a k) -> p h a k", a=2),
                                    axis=AX, op=ALU.add).then_inc(s["fd"], 1)
                    V.scalar_tensor_tensor(r_sb[:, :, 0:NK], r_sb[:, :, 0:NK], NEG, z_sb[:, :, 0:NK],
                                           ALU.is_equal, ALU.mult).then_inc(s["es"], 1)
                    dve.wait_ge(s["fd"], b + 1)
                    V.reciprocal(dinv[:, :, :], den[:, :, :]).then_inc(s["fe"], 1)

        @block.gpsimd
        def _(pool):
            V = nc.gpsimd
            TT = V.tensor_tensor
            V.memset(vhat[:, :], 1.0).then_inc(s["vone"], 1)
            V.memset(QS[:, :, :, :, :].rearrange("p c e r n -> p (c e r n)").bitcast(mybir.dt.uint32), 0).then_inc(s["qzero"], 1)
            V.memset(KS[:, :, :, :].rearrange("p a r n -> p (a r n)"), 1.0).then_inc(s["kone"], 1)
            V.memset(s_sb[:, :, :, NK:KP], NEG)
            V.memset(top4[:, :, TOP:8], NEG).then_inc(s["pad"], 1)

            def residues(c):
                for t, nm in enumerate(("q", "k")):
                    pool.wait_ge(s["hi_" + nm], c + 1)
                    if c >= 1:
                        pool.wait_ge(s["lo_" + nm], c)
                        pool.wait_ge(s["mid_" + nm], c)
                    TT(r32[:, t, :], q32[:, t, :], parts[:, c % 2, t, 0, :], ALU.subtract).then_inc(s["r_" + nm], 1)
                pool.wait_ge(s["mid_q"], c + 1)
                TT(parts[:, c % 2, 0, 2, :], r32[:, 0, :], parts[:, c % 2, 0, 1, :], ALU.subtract).then_inc(s["lo_q"], 1)

            residues(0)
            for slot in range(NSLOT):
                k = slot % 8
                b = slot // 8 - 1
                if slot < NC - 1:
                    residues(slot + 1)
                if slot == NC:
                    pool.wait_ge(s["w2"], NW2)
                    pool.wait_ge(s["xn"], NC)
                    TT(x_sb[:, :, :], x_sb[:, :, :], bo_sb[:, :].unsqueeze(1).to_broadcast([P, NT, D]), ALU.add)\
                        .then_inc(s["xb"], 1)
                if k in (3, 4) and 0 <= b < B:
                    t = k - 3
                    hs = slice(FH * t, FH * (t + 1))
                    pool.wait_ge(s["t8"], 2 * b + t + 1)
                    if b >= 1:
                        pool.wait_ge(s["mr"], 2 * b)
                    V.tensor_copy(top4[:, hs, 0:TOP], top8[:, hs, 1, 0:TOP]).then_inc(s["t4"], 1)
                if k == 4 and 0 <= b < B:
                    pool.wait_ge(s["fs_ev"], 2 * b + 2)
                    if b == 0:
                        pool.wait_ge(s["rn"], 1)
                    if b >= 1:
                        pool.wait_ge(s["es"], b)
                        pool.wait_ge(s["fd"], b)
                        pool.wait_ge(s["p0"], b)
                    rb = rn[:, BT * b:BT * (b + 1), :].rearrange("p t (h a) -> p (t h) a", a=2)

                    def per(a, n):
                        return rb[:, :, a:a + 1].to_broadcast([P, NH, n])
                    TT(z_sb[:, :, NK:NK + TOP], s_sb[:, :, 0, 0:TOP], per(0, TOP), ALU.mult)
                    TT(z_sb[:, :, NK + TOP:NK + 2 * TOP], top8[:, :, 0, 0:TOP], per(0, TOP), ALU.mult)
                    TT(z_sb[:, :, NK + 2 * TOP:ZW], top8[:, :, 1, 0:TOP], per(1, TOP), ALU.mult)
                    TT(z_sb[:, :, 0:NK], s_sb[:, :, 1, 0:NK], per(1, NK), ALU.mult).then_inc(s["z"], 1)
                    first = s_sb[:, :, 0, 0:TOP]
                    best = top8[:, :, 0, 0:TOP]
                    TT(cmp[:, :, :, :], best.unsqueeze(2).to_broadcast([P, NH, TOP, TOP]),
                       first.unsqueeze(3).to_broadcast([P, NH, TOP, TOP]), ALU.subtract).then_inc(s["cmp"], 1)
                    TT(ties[:, :, 0:3], first[:, :, 1:4], first[:, :, 0:3], ALU.subtract)
                    TT(ties[:, :, 3:5], first[:, :, 2:4], first[:, :, 0:2], ALU.subtract)
                    TT(ties[:, :, 5:6], first[:, :, 3:4], first[:, :, 0:1], ALU.subtract).then_inc(s["tie"], 1)
                    pool.wait_ge(s["cmp"], 2 * b + 1)
                    V.tensor_scalar(cmp[:, :, :, :], cmp[:, :, :, :], 0.0, None, ALU.is_gt).then_inc(s["cmp"], 1)
                    pool.wait_ge(s["tie"], 2 * b + 1)
                    V.tensor_scalar(ties[:, :, :], ties[:, :, :], 0.0, None, ALU.is_equal).then_inc(s["tie"], 1)
                    pool.wait_ge(s["cmp"], 2 * b + 2)
                    TT(cm2[:, :, :, :], cmp[:, :, :, 0:2], cmp[:, :, :, 2:4], ALU.add).then_inc(s["c2"], 1)
                    pool.wait_ge(s["c2"], b + 1)
                    TT(rank[:, 0, :, :], cm2[:, :, :, 0], cm2[:, :, :, 1], ALU.add).then_inc(s["rk"], 1)
                    pool.wait_ge(s["tie"], 2 * b + 2)
                    for i, (lo, n, at) in enumerate(((1, 3, 0), (2, 2, 3), (3, 1, 5))):
                        pool.wait_ge(s["rk"], 4 * b + i + 1)
                        TT(rank[:, 0, :, lo:TOP], rank[:, 0, :, lo:TOP], ties[:, :, at:at + n], ALU.add).then_inc(s["rk"], 1)
                    pool.wait_ge(s["rk"], 4 * b + 4)
                    V.tensor_scalar(rank[:, 1, :, :], rank[:, 0, :, :], float(TOP), None, ALU.is_lt).then_inc(s["sel"], 1)
                if k == 6 and 0 <= b < B:
                    pool.wait_ge(s["ze"], b + 1)
                    pool.wait_ge(s["sel"], b + 1)
                    TT(p0[:, :, :], rank[:, 1, :, :], z_sb[:, :, NK:NK + TOP], ALU.mult).then_inc(s["p0"], 1)
                    pool.wait_ge(s["p0"], b + 1)
                    TT(p0s[:, :, :], p0[:, :, 0:2], p0[:, :, 2:4], ALU.add).then_inc(s["ps"], 1)
                    pool.wait_ge(s["ps"], b + 1)
                    TT(p0r[:, 0, :], p0s[:, :, 0], p0s[:, :, 1], ALU.add).then_inc(s["p1"], 1)
                    pool.wait_ge(s["fe"], b + 1)
                    TT(dd[:, :], dinv[:, :, 0], dinv[:, :, 1], ALU.mult).then_inc(s["dd"], 1)
                    pool.wait_ge(s["p1"], b + 1)
                    TT(p0r[:, 1, :], den[:, :, 0], p0r[:, 0, :], ALU.subtract).then_inc(s["p2"], 1)
                    pool.wait_ge(s["dd"], b + 1)
                    TT(a0[:, :, :], p0[:, :, :], dd[:, :].unsqueeze(2).to_broadcast([P, NH, TOP]), ALU.mult)\
                        .then_inc(s["fa"], 1)
                    pool.wait_ge(s["p2"], b + 1)
                    TT(p0r[:, 2, :], p0r[:, 1, :], dinv[:, :, 0], ALU.mult).then_inc(s["rest"], 1)
                if k in (6, 7) and 0 <= b < B:
                    t = k - 6
                    pool.wait_ge(s["fa"], b + 1)
                    pool.wait_ge(s["es"], b + 1)
                    if b >= 1:
                        pool.wait_ge(s["wt"], b)
                    hs = slice(FH * t, FH * (t + 1))
                    TT(prod[:, t, :, :, :], r_sb[:, hs, 0:NK].unsqueeze(2).to_broadcast([P, FH, TOP, NK]),
                       a0[:, hs, :].unsqueeze(3).to_broadcast([P, FH, TOP, NK]), ALU.mult).then_inc(s["pr"], 1)
                    if t == 1:
                        pool.wait_ge(s["pr"], 4 * b + 2)
                        pool.wait_ge(s["rest"], b + 1)
                        lastx = prod[:, :, :, TOP - 1, NK - 1]
                        TT(lastx, lastx, p0r[:, 2, :].rearrange("p (t h) -> p t h", t=BT), ALU.add).then_inc(s["pr"], 1)
                        pool.wait_ge(s["pr"], 4 * b + 3)
                        TT(prod[:, :, 0:FH // 2, :, :].rearrange("p t h i j -> p t (h i j)"),
                           prod[:, :, 0:FH // 2, :, :].rearrange("p t h i j -> p t (h i j)"),
                           prod[:, :, FH // 2:FH, :, :].rearrange("p t h i j -> p t (h i j)"), ALU.add).then_inc(s["pr"], 1)


NAMES = ["L0_attn_x", "L0_attn_Wq", "L0_attn_bq", "L0_attn_Wl", "L0_attn_bl", "L0_attn_Wk", "L0_attn_bk",
         "L0_attn_Wv", "L0_attn_bv", "L0_attn_Wo", "L0_attn_bo", "L0_ffn_Wq", "L0_ffn_bq", "L0_ffn_bn_gamma",
         "L0_ffn_bn_beta", "L0_ffn_sub_key0", "L0_ffn_sub_key1", "L0_ffn_expert_down", "L0_ffn_expert_up"]


def kernel(**inputs):
    import concourse.bacc as bacc
    from concourse.bass_utils import run_bass_kernel_spmd

    nc = bacc.Bacc("TRN2", target_bir_lowering=False, num_devices=1)
    arrays, args = {}, []
    for name in NAMES:
        a = np.ascontiguousarray(inputs[name])
        arrays[name] = a
        args.append(nc.dram_tensor(name, a.shape, mybir.dt.from_np(a.dtype), kind="ExternalInput").ap())
    arrays["const"] = constants()
    args.append(nc.dram_tensor("const", (P, C_END), F32, kind="ExternalInput").ap())
    shape = inputs["L0_attn_x"].shape
    args.append(nc.dram_tensor("qk_parts", (2, shape[0] // 2, 16, 3, 8, 512), BF16, kind="Internal").ap())
    args.append(nc.dram_tensor("out", shape, F32, kind="ExternalOutput").ap())
    program(nc, *args)
    return run_bass_kernel_spmd(nc, [arrays], core_ids=[0]).results[0]["out"]
```
